# Optimizing a Trainium2 kernel written in Bass

```python
import numpy as np
import jax
import jax.numpy as jnp

def _softmax(x, axis=-1):
    return jax.nn.softmax(x, axis=axis)

def _gelu(x):
    return jax.nn.gelu(x, approximate=True)

def _silu(x):
    return jax.nn.silu(x)

def _sigmoid(x):
    return jax.nn.sigmoid(x)

def _layernorm(x, axis=-1, eps=1e-05):
    m = jnp.mean(x, axis=axis, keepdims=True)
    v = jnp.var(x, axis=axis, keepdims=True)
    return (x - m) / jnp.sqrt(v + eps)

def _scatter_add(tgt, idx, src, axis=0):
    return tgt.at[idx].add(src)

def _segment_sum(src, seg, n):
    return jax.ops.segment_sum(src, seg, n)
kernel_name = 'mk_cond_resid_d1_seqx_r4_586c96'

def setup_inputs(seed: int=0):
    np.random.seed(seed)
    _w = jnp.asarray

    def _rec_inputs():
        import jax
        import jax.numpy as jnp
        _rk = jax.random.key(seed)
        x = -0.0003929 + 0.9999 * jax.random.normal(jax.random.fold_in(_rk, 1), (128, 64, 1024), jnp.float32)
        _lenS = 64 - jax.random.randint(jax.random.fold_in(_rk, 7), (128,), 0, max(1, 64 // 4) + 1, jnp.int32)
        _lenS2 = 64 - jax.random.randint(jax.random.fold_in(_rk, 8), (128,), 0, max(1, 64 // 4) + 1, jnp.int32)
        cond_512 = 0.00782532 + 1.00527 * jax.random.normal(jax.random.fold_in(_rk, 11), (128, 128), jnp.float32)
        return (x, cond_512)
    x, cond_512 = _rec_inputs()

    def _L0_cond_setup():
        import jax, jax.numpy as jnp
        from jax import lax
        import numpy as np
        CIN, COUT, K, STYLE_DIM = (64, 64, 3, 128)
        N_LAYERS = 4
        TYPES = ('same', 'upsample', 'same', 'downsample')
        SCALE = 1.0 / float(np.sqrt(CIN * K ** 2))
        EPS = 1e-08
        _BK = np.array([1.0, 3.0, 3.0, 1.0], dtype=np.float32)
        BLUR_K = _BK / _BK.sum()

        def _blur(x, kern, pad):
            B, C, _ = x.shape
            xp = jnp.pad(x, ((0, 0), (0, 0), (pad[0], pad[1])))
            w = jnp.broadcast_to(kern.astype(x.dtype)[None, None, :], (C, 1, kern.shape[0]))
            return lax.conv_general_dilated(xp, w, (1,), 'VALID', feature_group_count=C, dimension_numbers=('NCH', 'OIH', 'NCH'))

        def _conv_same(x, w):
            p = (K - 1) // 2
            return lax.conv_general_dilated(x[None], w, (1,), [(p, p)], dimension_numbers=('NCH', 'OIH', 'NCH'))[0]

        def _conv_down(x, w):
            return lax.conv_general_dilated(x[None], w, (2,), 'VALID', dimension_numbers=('NCH', 'OIH', 'NCH'))[0]

        def _conv_up(x, w_t):
            return lax.conv_transpose(x[None], w_t, (2,), 'VALID', dimension_numbers=('NCH', 'IOH', 'NCH'), transpose_kernel=True)[0]

        def _layer(x, style, w, b, mw, mb, typ):
            s = style @ mw.T + mb
            weight = SCALE * w * s[:, None, :, None]
            demod = lax.rsqrt(jnp.sum(weight * weight, axis=(2, 3)) + EPS)
            weight = weight * demod[:, :, None, None]
            blur_k = jnp.asarray(BLUR_K)
            if typ == 'same':
                out = jax.vmap(_conv_same)(x, weight) + b[None, :, None]
            elif typ == 'upsample':
                out = jax.vmap(_conv_up)(x, weight.transpose(0, 2, 1, 3)) + b[None, :, None]
                out = _blur(out, 2.0 * blur_k, (1, 1))
            elif typ == 'downsample':
                xb = _blur(x, blur_k, (2, 2))
                out = jax.vmap(_conv_down)(xb, weight) + b[None, :, None]
            else:
                raise NotImplementedError(typ)
            return out
        key = jax.random.key(seed)
        ks = jax.random.split(key, 6)
        B, L = (16, 1024)
        return {'x': jax.random.normal(ks[0], (B, CIN, L), dtype=jnp.float32), 'style': jax.random.normal(ks[1], (B, STYLE_DIM), dtype=jnp.float32), 'weights': jax.random.normal(ks[2], (N_LAYERS, COUT, CIN, K), dtype=jnp.float32), 'biases': jax.random.normal(ks[3], (N_LAYERS, COUT), dtype=jnp.float32) * 0.1, 'mod_w': jax.random.normal(ks[4], (N_LAYERS, CIN, STYLE_DIM), dtype=jnp.float32) / np.sqrt(STYLE_DIM), 'mod_b': 1.0 + 0.1 * jax.random.normal(ks[5], (N_LAYERS, CIN), dtype=jnp.float32)}
    _L0_cond_all = _L0_cond_setup()
    _L0_cond_in = {k: v for k, v in _L0_cond_all.items() if k in ('weights', 'biases', 'mod_w', 'mod_b')}
    del _L0_cond_all
    return {'x': x, 'cond_512': cond_512, 'L0_cond_weights': _L0_cond_in['weights'], 'L0_cond_biases': _L0_cond_in['biases'], 'L0_cond_mod_w': _L0_cond_in['mod_w'], 'L0_cond_mod_b': _L0_cond_in['mod_b']}

def reference(x, cond_512, L0_cond_weights, L0_cond_biases, L0_cond_mod_w, L0_cond_mod_b):
    import jax
    import jax.numpy as jnp

    def _L0_cond_ref(x, style, weights, biases, mod_w, mod_b):
        import jax, jax.numpy as jnp
        from jax import lax
        import numpy as np
        CIN, COUT, K, STYLE_DIM = (64, 64, 3, 128)
        N_LAYERS = 4
        TYPES = ('same', 'upsample', 'same', 'downsample')
        SCALE = 1.0 / float(np.sqrt(CIN * K ** 2))
        EPS = 1e-08
        _BK = np.array([1.0, 3.0, 3.0, 1.0], dtype=np.float32)
        BLUR_K = _BK / _BK.sum()

        def _blur(x, kern, pad):
            B, C, _ = x.shape
            xp = jnp.pad(x, ((0, 0), (0, 0), (pad[0], pad[1])))
            w = jnp.broadcast_to(kern.astype(x.dtype)[None, None, :], (C, 1, kern.shape[0]))
            return lax.conv_general_dilated(xp, w, (1,), 'VALID', feature_group_count=C, dimension_numbers=('NCH', 'OIH', 'NCH'))

        def _conv_same(x, w):
            p = (K - 1) // 2
            return lax.conv_general_dilated(x[None], w, (1,), [(p, p)], dimension_numbers=('NCH', 'OIH', 'NCH'))[0]

        def _conv_down(x, w):
            return lax.conv_general_dilated(x[None], w, (2,), 'VALID', dimension_numbers=('NCH', 'OIH', 'NCH'))[0]

        def _conv_up(x, w_t):
            return lax.conv_transpose(x[None], w_t, (2,), 'VALID', dimension_numbers=('NCH', 'IOH', 'NCH'), transpose_kernel=True)[0]

        def _layer(x, style, w, b, mw, mb, typ):
            s = style @ mw.T + mb
            weight = SCALE * w * s[:, None, :, None]
            demod = lax.rsqrt(jnp.sum(weight * weight, axis=(2, 3)) + EPS)
            weight = weight * demod[:, :, None, None]
            blur_k = jnp.asarray(BLUR_K)
            if typ == 'same':
                out = jax.vmap(_conv_same)(x, weight) + b[None, :, None]
            elif typ == 'upsample':
                out = jax.vmap(_conv_up)(x, weight.transpose(0, 2, 1, 3)) + b[None, :, None]
                out = _blur(out, 2.0 * blur_k, (1, 1))
            elif typ == 'downsample':
                xb = _blur(x, blur_k, (2, 2))
                out = jax.vmap(_conv_down)(xb, weight) + b[None, :, None]
            else:
                raise NotImplementedError(typ)
            return out
        out = x
        for i, typ in enumerate(TYPES):
            out = _layer(out, style, weights[i], biases[i], mod_w[i], mod_b[i], typ)
        return out
    x = x + _L0_cond_ref(x, cond_512, L0_cond_weights, L0_cond_biases, L0_cond_mod_w, L0_cond_mod_b)
    return x

_drawn_inputs = setup_inputs


def setup_inputs(seed=0):
    import zlib

    import numpy as np

    out = dict(_drawn_inputs(seed))
    spreads = {}
    factors = {}
    for name, (base, spread) in spreads.items():
        noise = np.random.default_rng([zlib.crc32(name.encode()), seed]).standard_normal(out[name].shape)
        drawn = base * np.exp(spread * noise) if base else spread * noise
        out[name] = jnp.asarray(drawn.astype(out[name].dtype))
    for name, factor in factors.items():
        out[name] = (out[name] * factor).astype(out[name].dtype)
    return out
```

```python
from contextlib import ExitStack

import concourse.bass as bass
from concourse import mybir

ALU = mybir.AluOpType
ACT = mybir.ActivationFunctionType
F32 = mybir.dt.float32
F32R = mybir.dt.float32r

B = 128
C = 64
NG = 8
NGR = B // NG
Q = 4
NQ = B // Q
EC = 32
K = 513
XR = 3
TR = 2
EPS = 1e-8 * (C * 9)
STAGE_A = [[(0, 0)], [(0, 1), (1, 0)], [(1, 1)]]
STAGE_B = [[0, 1], [0, 1, 2], [0, 1, 2], [2]]
PIECE_SLOT = [0, 0, 1, 2, 3, 4, 5]


def build(nc, xin, xe, l0, a2, b1, q3, ed, wt, mwt, bb, st, out):
    with ExitStack() as ctx:
        def sb(name, shape, dt=F32):
            return ctx.enter_context(nc.sbuf_tensor(name, shape, dt))

        def sem(name):
            return ctx.enter_context(nc.semaphore(name))

        X = sb("X", [128, XR, Q, K])
        T = sb("T", [128, TR, Q, K])
        xh = sb("xh", [128, 2, K + 1], F32R)
        xl = sb("xl", [128, 2, K + 1], F32R)
        zh = sb("zh", [128, 2, 516], F32R)
        zl = sb("zl", [128, 2, 516], F32R)
        Wh = sb("Wh", [128, 2, 4, NG, 2, C], F32R)
        Wl = sb("Wl", [128, 2, 4, NG, 2, C], F32R)
        GT = sb("GT", [128, 4, NG * C])
        Q2f = sb("Q2f", [128, 3, NG * C])
        Q2h = sb("Q2h", [128, 3, NG * C], F32R)
        Q2l = sb("Q2l", [128, 3, NG * C], F32R)
        Q3f = sb("Q3f", [128, 2, NG * C])
        Q3h = sb("Q3h", [128, 2, NG * C], F32R)
        Q3l = sb("Q3l", [128, 2, NG * C], F32R)
        L0f = sb("L0f", [128, 256])
        L0h = sb("L0h", [128, 256], F32R)
        L0l = sb("L0l", [128, 256], F32R)
        A2f = sb("A2f", [128, 256])
        A2h = sb("A2h", [128, 256], F32R)
        A2l = sb("A2l", [128, 256], F32R)
        B1h = sb("B1h", [128, 6, 2, C], F32R)
        B1l = sb("B1l", [128, 6, 2, C], F32R)
        q3s = sb("q3s", [128, 2, C])
        E = sb("E", [128, 4, 3, 128])
        MW = sb("MW", [128, 4, 128])
        ST = sb("ST", [128, B])
        BB = sb("BB", [128, 2, 4])
        S = sb("S", [128, 4, B])
        AA = sb("AA", [128, 4, B])
        DD = sb("DD", [128, 4, B])
        tmp = sb("tmp", [128, 4, B])
        WSQ = sb("WSQ", [64, 4, 128])
        WSM = sb("WSM", [64, 2, 128])
        D10 = sb("D10", [128, B])
        D21 = sb("D21", [128, B])
        D32 = sb("D32", [128, B])
        b0z = sb("b0z", [128, B])
        hb = sb("hb", [128, B])
        cv = sb("cv", [128, B])
        XE = sb("XE", [128, B, 7])
        XS = sb("XS", [128, EC, 7])
        ZE = sb("ZE", [128, EC, 6])
        Y = sb("Y", [128, EC, 10])
        Y1 = sb("Y1", [128, EC, 9])
        Y2 = sb("Y2", [128, EC, 8])
        U = sb("U", [128, EC, 8])
        HH = sb("HH", [128, EC, 8])
        XB = sb("XB", [128, EC, 5])
        EP = sb("EP", [128, B, 2])
        WT = T[0:64, 0, 0:3, 0:512]
        b1s = GT[:, 0:3, :].rearrange("p v n -> p (v n)")[:, 0:13 * C].rearrange("p (s i) -> p s i", i=C)
        RR = Q2f[:, 0, :].rearrange("p (l b) -> p l b", l=4)
        b1w = GT[:, 0:3, :].rearrange("p v n -> p (v n)")
        def psum(name):
            return ctx.enter_context(nc.psum_tensor(name, [128, 512], F32))

        pz = [psum("pz0"), psum("pz1")]
        po = [psum("po0"), psum("po1")]
        pc = [psum("pc0"), psum("pc1")]
        pe_ = psum("pe")
        ps = psum("ps")

        s_in = {n: sem("i_" + n) for n in ("mwt", "st", "bb", "wt", "q3", "a2", "l0", "b1", "ed", "xe")}
        s_x = [sem(f"x{i}") for i in range(XR)]
        s_st = [sem(f"st{i}") for i in range(TR)]
        s_wc = sem("wc")
        s_xh, s_xl, s_zh, s_zl = sem("xh"), sem("xl"), sem("zh"), sem("zl")
        s_z, s_o, s_t = sem("z"), sem("o"), sem("t")
        s_fin = sem("fin")
        s_c, s_ce = sem("c"), sem("ce")
        s_q3f, s_q3h, s_q3l = sem("q3f"), sem("q3h"), sem("q3l")
        s_q2h, s_q2l, s_wh, s_wl = sem("q2h"), sem("q2l"), sem("wh"), sem("wl")
        s_e, s_ed = sem("e"), sem("ed")
        s_pp, s_ch = sem("pp"), sem("ch")
        s_ms = sem("ms")
        s_sq = sem("sq")
        s_sc, s_wh0 = sem("sc"), sem("wh0")

        SC_SQ, SC_A, SC_D, SC_L0, SC_A2, SC_HB1, SC_HB2, SC_CV, SC_B1F, SC_B1 = range(1, 11)
        r32 = lambda ap: ap.bitcast(F32)

        def bc(ap, n):
            return ap.unsqueeze(2).to_broadcast([ap.shape[0], ap.shape[1], n])

        def split_mm(eng, o, wh_, wl_, rh, rl, first, last):
            eng.matmul(o, wh_, rh, start=first, stop=False)
            eng.matmul(o, wh_, rl, start=False, stop=False)
            return eng.matmul(o, wl_, rh, start=False, stop=last)

        gslice = lambda ap, g: ap[:, g * NG:(g + 1) * NG]
        g3 = lambda ap: ap.rearrange("p (b o) -> p b o", b=NG)
        groups_edge = {}
        for k in range(4):
            groups_edge[(0, k)] = (0, k)
        for c in range(1, B // EC):
            for k in range(4):
                groups_edge[(EC // NG * c - 1, 2 * k)] = (c, k)

        block = ctx.enter_context(nc.Block())

        @block.sync
        def _(sp):
            for n, dst, src in (("mwt", MW[:], mwt.rearrange("p (l m) -> p l m", l=4)),
                                ("bb", BB[:], bb.rearrange("p (k l) -> p k l", k=2)),
                                ("q3", q3s[:], q3.rearrange("p (k o) -> p k o", k=2)),
                                ("l0", L0f[:], l0)):
                sp.dma_start(dst, src).then_inc(s_in[n], 16)

            def load(n):
                if n >= XR:
                    sp.wait_ge(s_fin, n - XR + 1)
                sp.dma_start(X[:, n % XR], xin[n * Q:(n + 1) * Q].rearrange("b p k -> p b k")
                             ).then_inc(s_x[n % XR], 16)

            def store(n):
                sp.wait_ge(s_fin, n + 1)
                sp.dma_start(out[n * Q:(n + 1) * Q].rearrange("b p k -> p b k"), T[:, n % TR]
                             ).then_inc(s_st[n % TR], 16)

            load(0)
            sp.dma_start(XE[:], xe).then_inc(s_in["xe"], 16)
            for n in range(1, XR):
                load(n)
            for n in range(NQ):
                store(n)
                if n + XR < NQ:
                    load(n + XR)
            for i in range(TR):
                sp.wait_ge(s_st[i], 16 * len(range(i, NQ, TR)))

        @block.tensor
        def _(pe):
            def conv_z(b):
                pe.wait_ge(s_xh, b + 1)
                pe.wait_ge(s_xl, b + 1)
                if b >= 2:
                    pe.wait_ge(s_zh, b - 1)
                    pe.wait_ge(s_zl, b - 1)
                for j in range(2):
                    m = split_mm(pe, pz[b % 2][:, :], L0h[:, 128 * j:128 * j + 128], L0l[:, 128 * j:128 * j + 128],
                                 xh[:, b % 2, j:j + 512], xl[:, b % 2, j:j + 512], j == 0, j == 1)
                m.then_inc(s_z, 1)

            def conv_o(b):
                g, i = divmod(b, NG)
                if i == 0:
                    pe.wait_ge(s_wh, 4 * (g + 1))
                    pe.wait_ge(s_wl, 4 * (g + 1))
                    pe.wait_ge(s_wc, 4 * (g + 1))
                pe.wait_ge(s_zh, b + 1)
                pe.wait_ge(s_zl, b + 1)
                if b >= 2:
                    pe.wait_ge(s_t, b - 1)
                for j in range(4):
                    w = [t[:, g % 2, j, i].rearrange("p r o -> p (r o)") for t in (Wh, Wl)]
                    m = split_mm(pe, po[b % 2][:, :], w[0], w[1], zh[:, b % 2, j:j + 512], zl[:, b % 2, j:j + 512],
                                 j == 0, j == 3)
                m.then_inc(s_o, 1)

            def piece(g, k):
                n = 7 * g + k
                o = pc[n % 2][:, :]
                if n >= 2:
                    pe.wait_ge(s_ce, n - 1)
                if k == 0:
                    pe.wait_ge(s_q3h, g + 1)
                    pe.wait_ge(s_q3l, g + 1)
                if k < 3:
                    prods = STAGE_A[k]
                    for x, (p, d) in enumerate(prods):
                        m = split_mm(pe, o, A2h[:, 128 * d:128 * d + 128], A2l[:, 128 * d:128 * d + 128],
                                     Q3h[:, p, :], Q3l[:, p, :], x == 0, x == len(prods) - 1)
                else:
                    v = k - 3
                    need = 3 * g + STAGE_B[v][-1] + 1
                    pe.wait_ge(s_q2h, need)
                    pe.wait_ge(s_q2l, need)
                    for x, p in enumerate(STAGE_B[v]):
                        w = [t[:, 2 * v - p + 1].rearrange("p r i -> p (r i)") for t in (B1h, B1l)]
                        m = split_mm(pe, o, w[0], w[1],
                                     Q2h[:, p, :], Q2l[:, p, :], x == 0, x == len(STAGE_B[v]) - 1)
                m.then_inc(s_c, 1)

            def edge(c, k):
                pe.wait_ge(s_ed, 5 * c + k + 1)
                if k == 0:
                    for t in range(3):
                        m = pe.matmul(pe_[:, 0:5 * EC], E[:, 0, t, :], XS[:, :, t:t + 5], start=t == 0, stop=t == 2)
                elif k == 1:
                    pe.matmul(pe_[:, 0:5 * EC], E[:, 1, 0, :], ZE[:, :, 1:6], start=True, stop=False)
                    pe.matmul(pe_[:, 0:5 * EC], E[:, 1, 2, :], ZE[:, :, 0:5], start=False, stop=True)
                    m = pe.matmul(pe_[:, 5 * EC:9 * EC], E[:, 1, 1, :], ZE[:, :, 1:5], start=True, stop=True)
                elif k == 2:
                    for t in range(3):
                        m = pe.matmul(pe_[:, 0:6 * EC], E[:, 2, t, :], U[:, :, t:t + 6], start=t == 0, stop=t == 2)
                else:
                    for t in range(3):
                        m = pe.matmul(pe_[:, 0:2 * EC], E[:, 3, t, :], XB[:, :, t:t + 3:2], start=t == 0, stop=t == 2)
                m.then_inc(s_e, 1)

            for n in ("mwt", "st"):
                pe.wait_ge(s_in[n], 16)
            for l in range(4):
                m = pe.matmul(ps[:, l * 128:l * 128 + 128], MW[:, l, :], ST[:, :], start=True, stop=True)
            m.then_inc(s_pp, 1)
            pe.wait_ge(s_sc, SC_SQ)
            for l in range(4):
                m = pe.matmul(ps[:, l * 128:l * 128 + 128], WSQ[:, l, :], tmp[0:64, l, :], start=True, stop=True)
            m.then_inc(s_pp, 1)
            pe.wait_ge(s_sc, SC_A2)
            pe.wait_ge(s_wh0, 2)
            piece(0, 0)
            piece(0, 1)
            conv_z(0)
            piece(0, 2)
            pe.wait_ge(s_sc, SC_HB1)
            pe.matmul(ps[:, 0:128], WSM[:, 0, :], tmp[0:64, 0, :], start=True, stop=True).then_inc(s_pp, 1)
            pe.wait_ge(s_sc, SC_HB2)
            pe.matmul(ps[:, 128:256], WSM[:, 1, :], tmp[0:64, 1, :], start=True, stop=True).then_inc(s_pp, 1)
            pe.wait_ge(s_sc, SC_B1)
            for k in range(3, 7):
                piece(0, k)
            pe.wait_ge(s_in["ed"], 16)
            for b in range(B):
                g, i = divmod(b, NG)
                if b + 1 < B:
                    conv_z(b + 1)
                conv_o(b)
                if g + 1 < NGR:
                    for k in range(7):
                        if PIECE_SLOT[k] == i:
                            piece(g + 1, k)
                if (g, i) in groups_edge:
                    edge(*groups_edge[(g, i)])

        @block.scalar
        def _(act):
            for n, dst, src in (("st", ST[:], st),
                                ("wt", WT, wt.rearrange("p (l m) -> p l m", l=3)),
                                ("a2", A2f[:], a2),
                                ("b1", b1w[:, 0:19 * C], b1),
                                ("ed", E[:], ed.rearrange("p (l t m) -> p l t m", l=4, t=3))):
                act.dma_start(dst, src).then_inc(s_in[n], 16)

            def x_high(b):
                n = b // Q
                if b % Q == 0:
                    act.wait_ge(s_x[n % XR], 16 * (n // XR + 1))
                if b >= 2:
                    act.wait_ge(s_z, b - 1)
                act.activation(xh[:, b % 2, 0:K], X[:, n % XR, b % Q, :], ACT.Identity,
                               scale=S[:, 0, b:b + 1]).then_inc(s_xh, 1)

            def z_high(b):
                act.wait_ge(s_z, b + 1)
                if b >= 2:
                    act.wait_ge(s_o, b - 1)
                act.activation(zh[:, b % 2, 1:513], pz[b % 2][:, :], ACT.Identity,
                               bias=b0z[:, b:b + 1]).then_inc(s_zh, 1)

            def t_out(b):
                n = b // Q
                act.wait_ge(s_o, b + 1)
                if b % Q == 0 and n >= TR:
                    act.wait_ge(s_st[n % TR], 16 * (n // TR))
                act.activation(T[:, n % TR, b % Q, 1:K], po[b % 2][:, :], ACT.Identity,
                               bias=cv[:, b:b + 1], scale=DD[:, 3, b:b + 1]).then_inc(s_t, 1)

            def q3_high(g):
                act.wait_ge(s_q3f, g + 1)
                if g:
                    act.wait_ge(s_c, 7 * (g - 1) + 3)
                act.copy(Q3h[:, :, :], Q3f[:, :, :]).then_inc(s_q3h, 1)

            def piece(g, k):
                act.wait_ge(s_ce, 7 * g + k + 1)
                if k < 3:
                    if g:
                        act.wait_ge(s_c, 7 * g)
                    act.copy(Q2h[:, k, :], Q2f[:, k, :]).then_inc(s_q2h, 1)
                else:
                    if g >= 2 and k == 3:
                        act.wait_ge(s_o, NG * (g - 1))
                    act.copy(Wh[:, g % 2, k - 3, :, 0, :], g3(GT[:, k - 3, :])).then_inc(s_wh, 1)

            act.wait_ge(s_in["l0"], 16)
            act.copy(L0h[:], L0f[:]).then_inc(s_wh0, 1)
            act.wait_ge(s_in["a2"], 16)
            act.copy(A2h[:], A2f[:]).then_inc(s_wh0, 1)
            act.wait_ge(s_sc, SC_A)
            act.activation(RR, AA[:], ACT.Sqrt).then_inc(s_sq, 1)
            act.wait_ge(s_ms, 1)
            q3_high(0)
            x_high(0)
            piece(0, 0)
            piece(0, 1)
            x_high(1)
            z_high(0)
            piece(0, 2)
            act.wait_ge(s_sc, SC_B1F)
            for h in range(2):
                act.mul(B1h[:, :, h, :], b1s[:, 2 * h:2 * h + 11:2, :], 1.0 / 32.0).then_inc(s_wh0, 1)
            for k in range(3, 7):
                piece(0, k)
            q3_high(1)
            act.wait_ge(s_sc, SC_B1)
            for b in range(B):
                g, i = divmod(b, NG)
                if b + 2 < B:
                    x_high(b + 2)
                if b + 1 < B:
                    z_high(b + 1)
                if g + 1 < NGR:
                    for k in range(7):
                        if PIECE_SLOT[k] == i - 1:
                            piece(g + 1, k)
                if i == 6 and g + 2 < NGR:
                    q3_high(g + 2)
                t_out(b)

        @block.gpsimd
        def _(pool):
            pool.memset(r32(zh[:]), 0.0)
            pool.memset(r32(zl[:]), 0.0)
            for d in range(2):
                pool.memset(r32(Wh[0:64, d, 0, :, 1, :]), 0.0)
                pool.memset(r32(Wl[0:64, d, 0, :, 1, :]), 0.0)
            for t in (ZE, Y, U, HH):
                last = pool.memset(t[:], 0.0)
            last.then_inc(s_ms, 1)

            def q3(g):
                if g:
                    pool.wait_ge(s_q3h, g)
                    pool.wait_ge(s_q3l, g)
                for p in range(2):
                    m = pool.tensor_tensor(g3(Q3f[:, p, :]), q3s[:, p, :].unsqueeze(1).to_broadcast([128, NG, C]),
                                           bc(gslice(D32, g), C), ALU.mult)
                m.then_inc(s_q3f, 1)
                pool.wait_ge(s_q3h, g + 1)
                pool.tensor_tensor(Q3l[:, :, :], Q3f[:, :, :], r32(Q3h[:, :, :]), ALU.subtract).then_inc(s_q3l, 1)

            def piece(g, k):
                if k < 3:
                    pool.wait_ge(s_q2h, 3 * g + k + 1)
                    pool.tensor_tensor(Q2l[:, k, :], Q2f[:, k, :], r32(Q2h[:, k, :]), ALU.subtract
                                       ).then_inc(s_q2l, 1)
                else:
                    pool.wait_ge(s_wh, 4 * g + k - 2)
                    v, d = k - 3, g % 2
                    a, h = g3(GT[:, v, :]), r32(Wh[:, d, v, :, 0, :])
                    pool.tensor_tensor(Wl[:, d, v, :, 0, :], a, h, ALU.subtract).then_inc(s_wl, 1)

            pool.wait_ge(s_in["q3"], 16)
            pool.wait_ge(s_sc, SC_D)
            q3(0)
            for k in range(7):
                piece(0, k)
            pool.wait_ge(s_sc, SC_B1)
            for j in range(TR):
                pool.memset(T[0:64, j, :, 0:1], 0.0)
            q3(1)
            for b in range(B):
                g, i = divmod(b, NG)
                if g + 1 < NGR:
                    for k in range(7):
                        if PIECE_SLOT[k] == i - 1:
                            piece(g + 1, k)
                    if i == 6 and g + 2 < NGR:
                        q3(g + 2)

        @block.vector
        def _(dve):
            chain = [0]

            def link(ins):
                chain[0] += 1
                ins.then_inc(s_ch, 1)
                dve.wait_ge(s_ch, chain[0])

            def reached(ins):
                ins.then_inc(s_sc, 1)

            tt = dve.tensor_tensor
            bias = lambda l: BB[:, 0, l:l + 1]

            def x_low(b):
                dve.wait_ge(s_xh, b + 1)
                if b >= 2:
                    dve.wait_ge(s_z, b - 1)
                dve.scalar_tensor_tensor(out=xl[:, b % 2, 0:K], in0=X[:, b // Q % XR, b % Q, :],
                                         scalar=S[:, 0, b:b + 1], in1=r32(xh[:, b % 2, 0:K]),
                                         op0=ALU.mult, op1=ALU.subtract).then_inc(s_xl, 1)

            def z_low(b):
                dve.wait_ge(s_zh, b + 1)
                if b >= 2:
                    dve.wait_ge(s_o, b - 1)
                dve.scalar_tensor_tensor(out=zl[:, b % 2, 1:513], in0=pz[b % 2][:, :],
                                         scalar=b0z[:, b:b + 1], in1=r32(zh[:, b % 2, 1:513]),
                                         op0=ALU.add, op1=ALU.subtract).then_inc(s_zl, 1)

            def piece(g, k):
                n = 7 * g + k
                dve.wait_ge(s_c, n + 1)
                src = g3(pc[n % 2][:, :])
                if k < 3:
                    if g:
                        dve.wait_ge(s_q2h, 3 * (g - 1) + k + 1)
                        dve.wait_ge(s_q2l, 3 * (g - 1) + k + 1)
                    tt(g3(Q2f[:, k, :]), src, bc(gslice(D21, g), C), ALU.mult).then_inc(s_ce, 1)
                else:
                    if g:
                        dve.wait_ge(s_wh, 4 * (g - 1) + k - 2)
                        dve.wait_ge(s_wl, 4 * (g - 1) + k - 2)
                    tt(g3(GT[:, k - 3, :]), src, bc(gslice(D10, g), C), ALU.mult).then_inc(s_ce, 1)

            def cross(g, v):
                for t, s in ((Wh, s_wh), (Wl, s_wl)):
                    dve.wait_ge(s, 4 * g + v + 1)
                    if v < 3:
                        dve.tensor_copy(t[0:64, g % 2, v + 1, :, 1, :], r32(t[64:128, g % 2, v, :, 0, :]))
                    m = dve.tensor_copy(t[64:128, g % 2, v, :, 1, :], r32(t[0:64, g % 2, v, :, 0, :]))
                m.then_inc(s_wc, 1)

            def finish(n):
                dve.wait_ge(s_t, Q * (n + 1))
                dve.wait_ge(s_ed, 5 * (n * Q // EC) + 5)
                e = EP[:, n * Q:(n + 1) * Q, :]
                dve.tensor_copy(T[64:128, n % TR, :, 0:512:511], e[64:128])
                link(dve.tensor_copy(T[0:64, n % TR, :, 1:513:511], e[0:64]))
                tt(T[:, n % TR], T[:, n % TR], X[:, n % XR], ALU.add).then_inc(s_fin, 1)

            def edge_in(c):
                cs = slice(c * EC, (c + 1) * EC)
                tt(XS[:], XE[:, cs, :], bc(S[:, 0, cs], 7), ALU.mult).then_inc(s_ed, 1)

            def edge(c, k):
                cs = slice(c * EC, (c + 1) * EC)
                dve.wait_ge(s_e, 4 * c + k + 1)
                lo, hi = slice(0, 64), slice(64, 128)
                if k == 0:
                    v = Y1[:, :, 0:5]
                    link(tt(v, pe_[:, 0:5 * EC].rearrange("p (b n) -> p b n", n=5), bc(b0z[:, cs], 5), ALU.add))
                    tt(ZE[lo, :, 1:6], v[lo], bc(D10[lo, cs], 5), ALU.mult)
                    tt(ZE[hi, :, 0:5], v[hi], bc(D10[hi, cs], 5), ALU.mult).then_inc(s_ed, 1)
                elif k == 1:
                    v = Y1[:, :, :]
                    tt(v[:, :, 0:5], pe_[:, 0:5 * EC].rearrange("p (b n) -> p b n", n=5),
                       bc(S[:, 1, cs], 5), ALU.mult)
                    link(tt(v[:, :, 5:9], pe_[:, 5 * EC:9 * EC].rearrange("p (b n) -> p b n", n=4),
                            bc(S[:, 1, cs], 4), ALU.mult))
                    for h, o in ((lo, 1), (hi, 0)):
                        dve.tensor_scalar(Y[h, :, o:o + 9:2], v[h, :, 0:5], BB[h, 0, 1:2], None, ALU.add)
                        m = dve.tensor_scalar(Y[h, :, o + 1:o + 8:2], v[h, :, 5:9], BB[h, 0, 1:2], None, ALU.add)
                    link(m)
                    link(tt(Y1[:, :, 0:9], Y[:, :, 1:10], Y[:, :, 0:9], ALU.add))
                    link(tt(Y2[:, :, 0:8], Y1[:, :, 1:9], Y1[:, :, 0:8], ALU.add))
                    link(tt(Y1[:, :, 0:7], Y2[:, :, 1:8], Y2[:, :, 0:7], ALU.add))
                    for h, o in ((lo, 1), (hi, 0)):
                        m = dve.scalar_tensor_tensor(out=U[h, :, o:o + 7], in0=Y1[h, :, 0:7], scalar=0.25,
                                                     in1=bc(S[h, 2, cs], 7), op0=ALU.mult, op1=ALU.mult)
                    m.then_inc(s_ed, 1)
                elif k == 2:
                    v = Y1[:, :, 0:6]
                    link(tt(v, pe_[:, 0:6 * EC].rearrange("p (b n) -> p b n", n=6), bc(DD[:, 2, cs], 6), ALU.mult))
                    for h, o in ((lo, 2), (hi, 0)):
                        m = dve.tensor_scalar(HH[h, :, o:o + 6], v[h], BB[h, 0, 2:3], None, ALU.add)
                    link(m)
                    link(tt(Y1[:, :, 0:7], HH[:, :, 1:8], HH[:, :, 0:7], ALU.add))
                    link(tt(Y2[:, :, 0:6], Y1[:, :, 1:7], Y1[:, :, 0:6], ALU.add))
                    link(tt(Y1[:, :, 0:5], Y2[:, :, 1:6], Y2[:, :, 0:5], ALU.add))
                    dve.scalar_tensor_tensor(out=XB[:], in0=Y1[:, :, 0:5], scalar=0.125, in1=bc(S[:, 3, cs], 5),
                                             op0=ALU.mult, op1=ALU.mult).then_inc(s_ed, 1)
                else:
                    v = Y1[:, :, 0:2]
                    link(tt(v, pe_[:, 0:2 * EC].rearrange("p (b n) -> p b n", n=2), bc(DD[:, 3, cs], 2), ALU.mult))
                    for h, n in ((lo, 0), (hi, 1)):
                        dve.tensor_scalar(EP[hi, cs, n:n + 1], v[h, :, 0:1], BB[h, 0, 3:4], None, ALU.add)
                        m = dve.tensor_scalar(EP[lo, cs, n:n + 1], v[h, :, 1:2], BB[h, 0, 3:4], None, ALU.add)
                    m.then_inc(s_ed, 1)

            dve.wait_ge(s_in["wt"], 16)
            SQ = T[0:64, 1, 0:3, 0:512]
            link(tt(SQ, WT, WT, ALU.mult))
            SQ4 = [SQ[:, a, 128 * x:128 * x + 128] for a in range(3) for x in range(4)]
            W4 = [WT[:, a, 128 * x:128 * x + 128] for a in range(3) for x in range(4)]
            for l in range(4):
                m = tt(WSQ[:, l, :], SQ4[3 * l], SQ4[3 * l + 1], ALU.add)
            for l in range(2):
                m = tt(WSM[:, l, :], W4[3 * l + 6], W4[3 * l + 7], ALU.add)
            link(m)
            for l in range(4):
                m = tt(WSQ[:, l, :], WSQ[:, l, :], SQ4[3 * l + 2], ALU.add)
            for l in range(2):
                m = tt(WSM[:, l, :], WSM[:, l, :], W4[3 * l + 8], ALU.add)
            link(m)
            dve.wait_ge(s_in["bb"], 16)
            dve.wait_ge(s_pp, 1)
            psv = ps[:, :].rearrange("p (l b) -> p l b", l=4)
            link(tt(S[:], psv, bc(BB[:, 1, :], B), ALU.add))
            reached(tt(tmp[:], S[:], S[:], ALU.mult))
            dve.wait_ge(s_pp, 2)
            reached(dve.tensor_scalar(AA[:], psv, EPS, None, ALU.add))
            dve.wait_ge(s_sq, 1)
            link(dve.reciprocal(RR, RR))
            link(tt(tmp[:], RR, RR, ALU.mult))
            link(tt(tmp[:], tmp[:], AA[:], ALU.mult))
            link(dve.tensor_scalar(tmp[:], tmp[:], -0.5, 1.5, ALU.mult, ALU.add))
            link(tt(DD[:], tmp[:], RR, ALU.mult))
            tt(D32[:], DD[:, 2, :], S[:, 3, :], ALU.mult)
            tt(D21[:], S[:, 1, :], S[:, 2, :], ALU.mult)
            tt(D10[:], DD[:, 0, :], DD[:, 1, :], ALU.mult)
            link(tt(b0z[:], AA[:, 0, :], DD[:, 0, :], ALU.mult))
            reached(dve.tensor_scalar(b0z[:], b0z[:], bias(0), None, ALU.mult))
            dve.wait_ge(s_wh0, 1)
            reached(tt(L0l[:], L0f[:], r32(L0h[:]), ALU.subtract))
            dve.wait_ge(s_wh0, 2)
            reached(tt(A2l[:], A2f[:], r32(A2h[:]), ALU.subtract))
            x_low(0)
            piece(0, 0)
            piece(0, 1)
            x_low(1)
            dve.wait_ge(s_ms, 1)
            z_low(0)
            reached(dve.tensor_scalar(tmp[:, 0, :], S[:, 2, :], bias(1), 2.0, ALU.mult, ALU.mult))
            piece(0, 2)
            dve.wait_ge(s_pp, 3)
            link(tt(hb[:], ps[:, 0:128], DD[:, 2, :], ALU.mult))
            link(dve.tensor_scalar(hb[:], hb[:], bias(2), None, ALU.add))
            reached(tt(tmp[:, 1, :], hb[:], S[:, 3, :], ALU.mult))
            dve.wait_ge(s_pp, 4)
            link(tt(cv[:], ps[:, 128:256], DD[:, 3, :], ALU.mult))
            reached(dve.tensor_scalar(cv[:], cv[:], bias(3), None, ALU.add))
            dve.wait_ge(s_in["b1"], 16)
            src, dst = b1w, T[:, 1].rearrange("p q k -> p (q k)")
            for n in range(18, 12, -1):
                m = tt(dst[:, 0:n * C], src[:, C:(n + 1) * C], src[:, 0:n * C], ALU.add)
                if n > 13:
                    link(m)
                src, dst = dst, src
            reached(m)
            dve.wait_ge(s_wh0, 4)
            for h in range(2):
                m = dve.scalar_tensor_tensor(out=B1l[:, :, h, :], in0=b1s[:, 2 * h:2 * h + 11:2, :],
                                             scalar=1.0 / 32.0, in1=r32(B1h[:, :, h, :]),
                                             op0=ALU.mult, op1=ALU.subtract)
            reached(m)
            dve.wait_ge(s_sc, SC_B1)
            for k in range(3, 7):
                piece(0, k)
                cross(0, k - 3)
            dve.wait_ge(s_in["xe"], 16)
            edge_in(0)
            for b in range(B + 1):
                g, i = divmod(b, NG)
                if b + 2 < B:
                    x_low(b + 2)
                if b + 1 < B:
                    z_low(b + 1)
                if g + 1 < NGR:
                    for k in range(7):
                        if PIECE_SLOT[k] == i - 1:
                            piece(g + 1, k)
                    for k in range(3, 7):
                        if PIECE_SLOT[k] == i - 2:
                            cross(g + 1, k - 3)
                pg, pi = divmod(b - 1, NG)
                if (pg, pi) in groups_edge:
                    c, k = groups_edge[(pg, pi)]
                    edge(c, k)
                    if k == 3 and c + 1 < B // EC:
                        edge_in(c + 1)
                if b and b % Q == 0:
                    finish(b // Q - 1)



def layouts(x, cond_512, w, bia, mw, mb):
    import numpy as np
    f = np.float32
    B, C, L = x.shape
    xp = np.zeros((B, C, L + 2), f); xp[:, :, 1:L + 1] = x
    xin = np.ascontiguousarray(xp.reshape(B, C, L // 2 + 1, 2).transpose(0, 3, 1, 2)).reshape(B, 128, L // 2 + 1)
    xe = np.concatenate([xp[:, :, 0:7], xp[:, :, L - 5:L + 2]], axis=1).transpose(1, 0, 2)
    l0 = np.zeros((2, C, 2, 2, C), f)
    for j in range(2):
        for r in range(2):
            for h in range(2):
                t = 2 * j + r - h
                if 0 <= t < 3: l0[r, :, j, h, :] = w[0, :, :, t].T
    a2 = np.zeros((2, C, 4, C), f)
    for s in range(4):
        for r in range(2):
            if 0 <= s - r < 3: a2[r, :, s, :] = w[2, :, :, s - r]
    b1 = np.zeros((2, C, 19, C), f)
    for s in range(-8, 11):
        for r in range(2):
            if 0 <= s - r < 3: b1[r, :, s + 8, :] = w[1, :, :, 2 - (s - r)].T
    q3 = np.zeros((2, C, 2, C), f)
    for p in range(2):
        for r in range(2):
            if 2 * p + r < 3: q3[r, :, p, :] = w[3, :, :, 2 * p + r].T
    ed = np.zeros((2, C, 4, 3, 2, C), f)
    for s in range(2):
        ed[s, :, :, :, s, :] = w.transpose(2, 0, 3, 1)
        ed[s, :, 1, :, s, :] = w[1].transpose(0, 2, 1)
    wt = w.transpose(2, 0, 3, 1)
    wt = np.stack([wt, wt], axis=3)
    mwt = np.stack([mw.transpose(2, 0, 1)] * 2, axis=2)
    bb = np.stack([bia.T, mb.T], axis=1)
    bb = np.concatenate([bb, bb], axis=0)
    out = dict(xin=xin, xe=xe, l0=l0.reshape(128, 256), a2=a2.reshape(128, 256), b1=b1.reshape(128, 19 * 64),
               q3=q3.reshape(128, 128), ed=ed.reshape(128, 12 * 128), wt=wt.reshape(64, 12 * 128),
               mwt=mwt.reshape(128, 512), bb=bb.reshape(128, 8), st=cond_512.T)
    return {k: np.ascontiguousarray(v) for k, v in out.items()}


_ORDER = ["xin", "xe", "l0", "a2", "b1", "q3", "ed", "wt", "mwt", "bb", "st"]


def kernel(x, cond_512, L0_cond_weights, L0_cond_biases, L0_cond_mod_w, L0_cond_mod_b):
    import numpy as np
    import concourse.bacc as bacc
    from concourse.bass_utils import run_bass_kernel_spmd

    d = layouts(*(np.asarray(a) for a in (x, cond_512, L0_cond_weights, L0_cond_biases, L0_cond_mod_w,
                                          L0_cond_mod_b)))
    d["xe"] = d["xe"].reshape(128, B, 7)
    nc = bacc.Bacc("TRN2", target_bir_lowering=False, num_devices=1)
    arrays = {f"in_{n}": d[n] for n in _ORDER}
    args = [nc.dram_tensor(f"in_{n}", d[n].shape, F32, kind="ExternalInput").ap() for n in _ORDER]
    out = nc.dram_tensor("out_0", (B, 128, K), F32, kind="ExternalOutput").ap()
    build(nc, *args, out)
    r = run_bass_kernel_spmd(nc, [arrays], core_ids=[0])
    o = r.results[0]["out_0"].reshape(B, 2, C, K).transpose(0, 2, 3, 1).reshape(B, C, 2 * K)
    return np.ascontiguousarray(o[:, :, 1:2 * K - 1])
```

```python
from contextlib import ExitStack

import concourse.bass as bass
from concourse import mybir

ALU = mybir.AluOpType
ACT = mybir.ActivationFunctionType
F32 = mybir.dt.float32
F32R = mybir.dt.float32r

B = 128
C = 64
NG = 8
NGR = B // NG
Q = 4
NQ = B // Q
EC = 32
K = 513
XR = 3
TR = 2
EPS = 1e-8 * (C * 9)
STAGE_A = [[(0, 0)], [(0, 1), (1, 0)], [(1, 1)]]
STAGE_B = [[0, 1], [0, 1, 2], [0, 1, 2], [2]]
PIECE_SLOT = [0, 0, 1, 2, 3, 4, 5]


def build(nc, xin, xe, l0, a2, b1, q3, ed, wt, mwt, bb, st, out):
    with ExitStack() as ctx:
        def sb(name, shape, dt=F32):
            return ctx.enter_context(nc.sbuf_tensor(name, shape, dt))

        def sem(name):
            return ctx.enter_context(nc.semaphore(name))

        X = sb("X", [128, XR, Q, K])
        T = sb("T", [128, TR, Q, K])
        xh = sb("xh", [128, 2, K + 1], F32R)
        xl = sb("xl", [128, 2, K + 1], F32R)
        zh = sb("zh", [128, 2, 516], F32R)
        zl = sb("zl", [128, 2, 516], F32R)
        Wh = sb("Wh", [128, 2, 4, NG, 2, C], F32R)
        Wl = sb("Wl", [128, 2, 4, NG, 2, C], F32R)
        GT = sb("GT", [128, 4, NG * C])
        Q2f = sb("Q2f", [128, 3, NG * C])
        Q2h = sb("Q2h", [128, 3, NG * C], F32R)
        Q2l = sb("Q2l", [128, 3, NG * C], F32R)
        Q3f = sb("Q3f", [128, 2, NG * C])
        Q3h = sb("Q3h", [128, 2, NG * C], F32R)
        Q3l = sb("Q3l", [128, 2, NG * C], F32R)
        L0f = sb("L0f", [128, 256])
        L0h = sb("L0h", [128, 256], F32R)
        L0l = sb("L0l", [128, 256], F32R)
        A2f = sb("A2f", [128, 256])
        A2h = sb("A2h", [128, 256], F32R)
        A2l = sb("A2l", [128, 256], F32R)
        B1h = sb("B1h", [128, 6, 2, C], F32R)
        B1l = sb("B1l", [128, 6, 2, C], F32R)
        q3s = sb("q3s", [128, 2, C])
        E = sb("E", [128, 4, 3, 128])
        MW = sb("MW", [128, 4, 128])
        ST = sb("ST", [128, B])
        BB = sb("BB", [128, 2, 4])
        S = sb("S", [128, 4, B])
        AA = sb("AA", [128, 4, B])
        DD = sb("DD", [128, 4, B])
        tmp = sb("tmp", [128, 4, B])
        WSQ = sb("WSQ", [64, 4, 128])
        WSM = sb("WSM", [64, 2, 128])
        D10 = sb("D10", [128, B])
        D10c = sb("D10c", [128, B])
        D21 = sb("D21", [128, B])
        D32 = sb("D32", [128, B])
        b0z = sb("b0z", [128, B])
        hb = sb("hb", [128, B])
        cv = sb("cv", [128, B])
        XE = sb("XE", [128, B, 7])
        XS = sb("XS", [128, EC, 7])
        ZE = sb("ZE", [128, EC, 6])
        Y = sb("Y", [128, EC, 10])
        Y1 = sb("Y1", [128, EC, 9])
        Y2 = sb("Y2", [128, EC, 8])
        U = sb("U", [128, EC, 8])
        HH = sb("HH", [128, EC, 8])
        XB = sb("XB", [128, EC, 5])
        EP = sb("EP", [128, B, 2])
        WT = T[0:64, 0].rearrange("p q k -> p (q k)")[:, 0:1536].rearrange("p (l t m) -> p l t m", l=4, t=3)
        SQ = T[0:64, 1].rearrange("p q k -> p (q k)")[:, 0:1536].rearrange("p (l t m) -> p l t m", l=4, t=3)
        b1s = GT[:, 0:3, :].rearrange("p v n -> p (v n)")[:, 0:13 * C].rearrange("p (s i) -> p s i", i=C)
        b1p = Q2f[:, :, :].rearrange("p v n -> p (v n)")
        RR = GT[:, 3, :].rearrange("p (l b) -> p l b", l=4)
        b1w = GT[:, 0:3, :].rearrange("p v n -> p (v n)")
        def psum(name):
            return ctx.enter_context(nc.psum_tensor(name, [128, 512], F32))

        pz = [psum("pz0"), psum("pz1")]
        po = [psum("po0"), psum("po1")]
        pc = [psum("pc0"), psum("pc1")]
        pe_ = psum("pe")
        ps = psum("ps")

        s_in = {n: sem("i_" + n) for n in ("mwt", "st", "bb", "wt", "q3", "a2", "l0", "b1", "ed", "xe")}
        s_x = [sem(f"x{i}") for i in range(XR)]
        s_st = [sem(f"st{i}") for i in range(TR)]
        s_wx, s_wc = sem("wx"), sem("wc")
        s_xh, s_xl, s_zh, s_zl = sem("xh"), sem("xl"), sem("zh"), sem("zl")
        s_z, s_o, s_t = sem("z"), sem("o"), sem("t")
        s_fin = sem("fin")
        s_c, s_ce = sem("c"), sem("ce")
        s_q3f, s_q3h, s_q3l = sem("q3f"), sem("q3h"), sem("q3l")
        s_q2h, s_q2l, s_wh, s_wl = sem("q2h"), sem("q2l"), sem("wh"), sem("wl")
        s_e, s_ed = sem("e"), sem("ed")
        s_pp, s_ch = sem("pp"), sem("ch")
        s_ms = sem("ms")
        s_sq = sem("sq")
        s_sc, s_wh0 = sem("sc"), sem("wh0")
        s_b1 = sem("b1")

        SC_SQ2, SC_A2, SC_WL, SC_SQ, SC_A, SC_D, SC_HB1, SC_HB2, SC_CV = range(1, 10)
        r32 = lambda ap: ap.bitcast(F32)

        def bc(ap, n):
            return ap.unsqueeze(2).to_broadcast([ap.shape[0], ap.shape[1], n])

        def split_mm(eng, o, wh_, wl_, rh, rl, first, last):
            eng.matmul(o, wh_, rh, start=first, stop=False)
            eng.matmul(o, wh_, rl, start=False, stop=False)
            return eng.matmul(o, wl_, rh, start=False, stop=last)

        gslice = lambda ap, g: ap[:, g * NG:(g + 1) * NG]
        g3 = lambda ap: ap.rearrange("p (b o) -> p b o", b=NG)
        groups_edge = {}
        for k in range(4):
            groups_edge[(0, (0, 1, 3, 4)[k])] = (0, k)
        for c in range(1, B // EC):
            for k in range(4):
                groups_edge[(EC // NG * c - 1, 2 * k)] = (c, k)

        block = ctx.enter_context(nc.Block())

        @block.sync
        def _(sp):
            for n, dst, src in (("mwt", MW[:], mwt.rearrange("p (l m) -> p l m", l=4)),
                                ("bb", BB[:], bb.rearrange("p (k l) -> p k l", k=2)),
                                ("b1", b1w[:, 0:19 * C], b1),
                                ("q3", q3s[:], q3.rearrange("p (k o) -> p k o", k=2))):
                sp.dma_start(dst, src).then_inc(s_in[n], 16)

            def load(n):
                if n >= XR:
                    sp.wait_ge(s_fin, n - XR + 1)
                sp.dma_start(X[:, n % XR], xin[n * Q:(n + 1) * Q].rearrange("b p k -> p b k")
                             ).then_inc(s_x[n % XR], 16)

            def store(n):
                if n < NQ - 1:
                    sp.wait_ge(s_fin, n + 1)
                    sp.dma_start(out[n * Q:(n + 1) * Q].rearrange("b p k -> p b k"), T[:, n % TR]
                                 ).then_inc(s_st[n % TR], 16)
                    return
                for j in range(Q):
                    sp.wait_ge(s_fin, n + 1 + j)
                    sp.dma_start(out[n * Q + j], T[:, n % TR, j, :]).then_inc(s_st[n % TR], 16)

            load(0)
            sp.dma_start(XE[:], xe).then_inc(s_in["xe"], 16)
            for n in range(1, XR):
                load(n)
            for n in range(NQ):
                store(n)
                if n + XR < NQ:
                    load(n + XR)
            for i in range(TR):
                sp.wait_ge(s_st[i], 16 * (len(range(i, NQ, TR)) + (Q - 1 if (NQ - 1) % TR == i else 0)))

        @block.tensor
        def _(pe):
            def conv_z(b):
                pe.wait_ge(s_xh, b + 1)
                pe.wait_ge(s_xl, b + 1)
                if b >= 2:
                    pe.wait_ge(s_zh, b - 1)
                    pe.wait_ge(s_zl, b - 1)
                for j in range(2):
                    m = split_mm(pe, pz[b % 2][:, :], L0h[:, 128 * j:128 * j + 128], L0l[:, 128 * j:128 * j + 128],
                                 xh[:, b % 2, j:j + 512], xl[:, b % 2, j:j + 512], j == 0, j == 1)
                m.then_inc(s_z, 1)

            def conv_o(b):
                g, i = divmod(b, NG)
                if i == 0:
                    pe.wait_ge(s_wh, 4 * (g + 1))
                    pe.wait_ge(s_wl, 4 * (g + 1))
                    pe.wait_ge(s_wx, 4 * (g + 1))
                    pe.wait_ge(s_wc, 4 * (g + 1))
                pe.wait_ge(s_zh, b + 1)
                pe.wait_ge(s_zl, b + 1)
                if b >= 2:
                    pe.wait_ge(s_t, b - 1)
                for j in range(4):
                    w = [t[:, g % 2, j, i].rearrange("p r o -> p (r o)") for t in (Wh, Wl)]
                    m = split_mm(pe, po[b % 2][:, :], w[0], w[1], zh[:, b % 2, j:j + 512], zl[:, b % 2, j:j + 512],
                                 j == 0, j == 3)
                m.then_inc(s_o, 1)

            def piece(g, k):
                n = 7 * g + k
                o = pc[n % 2][:, :]
                if n >= 2:
                    pe.wait_ge(s_ce, n - 1)
                if k == 0:
                    pe.wait_ge(s_q3h, g + 1)
                    pe.wait_ge(s_q3l, g + 1)
                if k < 3:
                    prods = STAGE_A[k]
                    for x, (p, d) in enumerate(prods):
                        m = split_mm(pe, o, A2h[:, 128 * d:128 * d + 128], A2l[:, 128 * d:128 * d + 128],
                                     Q3h[:, p, :], Q3l[:, p, :], x == 0, x == len(prods) - 1)
                else:
                    v = k - 3
                    need = 3 * g + STAGE_B[v][-1] + 1
                    pe.wait_ge(s_q2h, need)
                    pe.wait_ge(s_q2l, need)
                    for x, p in enumerate(STAGE_B[v]):
                        w = [t[:, 2 * v - p + 1].rearrange("p r i -> p (r i)") for t in (B1h, B1l)]
                        m = split_mm(pe, o, w[0], w[1],
                                     Q2h[:, p, :], Q2l[:, p, :], x == 0, x == len(STAGE_B[v]) - 1)
                m.then_inc(s_c, 1)

            def edge(c, k):
                pe.wait_ge(s_ed, 5 * c + k + 1)
                if k == 0:
                    for t in range(3):
                        m = pe.matmul(pe_[:, 0:5 * EC], E[:, 0, t, :], XS[:, :, t:t + 5], start=t == 0, stop=t == 2)
                elif k == 1:
                    pe.matmul(pe_[:, 0:5 * EC], E[:, 1, 0, :], ZE[:, :, 1:6], start=True, stop=False)
                    pe.matmul(pe_[:, 0:5 * EC], E[:, 1, 2, :], ZE[:, :, 0:5], start=False, stop=True)
                    m = pe.matmul(pe_[:, 5 * EC:9 * EC], E[:, 1, 1, :], ZE[:, :, 1:5], start=True, stop=True)
                elif k == 2:
                    for t in range(3):
                        m = pe.matmul(pe_[:, 0:6 * EC], E[:, 2, t, :], U[:, :, t:t + 6], start=t == 0, stop=t == 2)
                else:
                    for t in range(3):
                        m = pe.matmul(pe_[:, 0:2 * EC], E[:, 3, t, :], XB[:, :, t:t + 3:2], start=t == 0, stop=t == 2)
                m.then_inc(s_e, 1)

            for n in ("mwt", "st"):
                pe.wait_ge(s_in[n], 16)
            for l in range(4):
                m = pe.matmul(ps[:, l * 128:l * 128 + 128], MW[:, l, :], ST[:, :], start=True, stop=True)
            m.then_inc(s_pp, 1)
            pe.wait_ge(s_sc, SC_SQ2)
            pe.matmul(ps[:, 256:384], WSQ[:, 2, :], tmp[0:64, 2, :], start=True, stop=True).then_inc(s_pp, 1)
            pe.wait_ge(s_sc, SC_SQ)
            for l in (0, 1, 3):
                m = pe.matmul(ps[:, l * 128:l * 128 + 128], WSQ[:, l, :], tmp[0:64, l, :], start=True, stop=True)
            m.then_inc(s_pp, 1)
            pe.wait_ge(s_wh0, 2)
            piece(0, 0)
            piece(0, 1)
            conv_z(0)
            piece(0, 2)
            pe.wait_ge(s_b1, 7)
            pe.wait_ge(s_wh0, 4)
            piece(0, 3)
            pe.wait_ge(s_sc, SC_HB1)
            pe.matmul(ps[:, 0:128], WSM[:, 0, :], tmp[0:64, 0, :], start=True, stop=True).then_inc(s_pp, 1)
            piece(0, 4)
            pe.wait_ge(s_sc, SC_HB2)
            pe.matmul(ps[:, 128:256], WSM[:, 1, :], tmp[0:64, 1, :], start=True, stop=True).then_inc(s_pp, 1)
            for k in range(5, 7):
                piece(0, k)
            pe.wait_ge(s_in["ed"], 16)
            for b in range(B):
                g, i = divmod(b, NG)
                if b + 1 < B:
                    conv_z(b + 1)
                conv_o(b)
                if g + 1 < NGR:
                    for k in range(7):
                        if PIECE_SLOT[k] == i:
                            piece(g + 1, k)
                if (g, i) in groups_edge:
                    edge(*groups_edge[(g, i)])

        @block.scalar
        def _(act):
            for n, dst, src in (("st", ST[:], st),
                                ("wt", WT, wt.rearrange("p (l t m) -> p l t m", l=4, t=3)),
                                ("a2", A2f[:], a2), ("l0", L0f[:], l0),
                                ("ed", E[:], ed.rearrange("p (l t m) -> p l t m", l=4, t=3))):
                act.dma_start(dst, src).then_inc(s_in[n], 16)

            def x_high(b):
                n = b // Q
                if b % Q == 0:
                    act.wait_ge(s_x[n % XR], 16 * (n // XR + 1))
                if b >= 2:
                    act.wait_ge(s_z, b - 1)
                act.activation(xh[:, b % 2, 0:K], X[:, n % XR, b % Q, :], ACT.Identity,
                               scale=S[:, 0, b:b + 1]).then_inc(s_xh, 1)

            def z_high(b):
                act.wait_ge(s_z, b + 1)
                if b >= 2:
                    act.wait_ge(s_o, b - 1)
                act.activation(zh[:, b % 2, 1:513], pz[b % 2][:, :], ACT.Identity,
                               bias=b0z[:, b:b + 1]).then_inc(s_zh, 1)

            def t_out(b):
                n = b // Q
                act.wait_ge(s_o, b + 1)
                if b % Q == 0 and n >= TR:
                    act.wait_ge(s_st[n % TR], 16 * (n // TR))
                act.activation(T[:, n % TR, b % Q, 1:K], po[b % 2][:, :], ACT.Identity,
                               bias=cv[:, b:b + 1], scale=DD[:, 3, b:b + 1]).then_inc(s_t, 1)

            def q3_high(g):
                act.wait_ge(s_q3f, g + 1)
                if g:
                    act.wait_ge(s_c, 7 * (g - 1) + 3)
                act.copy(Q3h[:, :, :], Q3f[:, :, :]).then_inc(s_q3h, 1)

            def piece(g, k):
                act.wait_ge(s_ce, 7 * g + k + 1)
                if k < 3:
                    if g:
                        act.wait_ge(s_c, 7 * g)
                    act.copy(Q2h[:, k, :], Q2f[:, k, :]).then_inc(s_q2h, 1)
                else:
                    if g >= 2 and k == 3:
                        act.wait_ge(s_o, NG * (g - 1))
                    v, w = k - 3, Wh[:, g % 2]
                    act.copy(w[:, v, :, 0, :], g3(GT[:, v, :])).then_inc(s_wh, 1)
                    if v < 3:
                        act.copy(w[0:64, v + 1, :, 1, :], g3(GT[64:128, v, :]))
                    act.copy(w[64:128, v, :, 1, :], g3(GT[0:64, v, :])).then_inc(s_wx, 1)

            act.wait_ge(s_in["l0"], 16)
            act.copy(L0h[:], L0f[:]).then_inc(s_wh0, 1)
            act.wait_ge(s_in["a2"], 16)
            act.copy(A2h[:], A2f[:]).then_inc(s_wh0, 1)
            act.wait_ge(s_sc, SC_A2)
            act.activation(RR[:, 2, :], AA[:, 2, :], ACT.Sqrt).then_inc(s_sq, 1)
            act.wait_ge(s_ms, 1)
            x_high(0)
            q3_high(0)
            act.wait_ge(s_sc, SC_A)
            act.activation(RR[:, 0:2, :], AA[:, 0:2, :], ACT.Sqrt)
            act.activation(RR[:, 3, :], AA[:, 3, :], ACT.Sqrt).then_inc(s_sq, 1)
            piece(0, 0)
            piece(0, 1)
            act.wait_ge(s_b1, 6)
            for h in range(2):
                act.copy(B1h[:, :, h, :], b1s[:, 2 * h:2 * h + 11:2, :]).then_inc(s_wh0, 1)
            piece(0, 2)
            act.wait_ge(s_sc, SC_D)
            z_high(0)
            x_high(1)
            for k in range(3, 7):
                piece(0, k)
            q3_high(1)
            act.wait_ge(s_sc, SC_CV)
            for b in range(B):
                g, i = divmod(b, NG)
                if b + 2 < B:
                    x_high(b + 2)
                if b + 1 < B:
                    z_high(b + 1)
                if g + 1 < NGR:
                    for k in range(7):
                        if PIECE_SLOT[k] == i - 1:
                            piece(g + 1, k)
                t_out(b)
                if i == 4 and g + 2 < NGR:
                    q3_high(g + 2)

        @block.gpsimd
        def _(pool):
            for t in (zh, zl):
                pool.memset(r32(t[:, :, 0:1]), 0.0)
                pool.memset(r32(t[:, :, 513:516]), 0.0)
            for d in range(2):
                pool.memset(r32(Wh[0:64, d, 0, :, 1, :]), 0.0)
                pool.memset(r32(Wl[0:64, d, 0, :, 1, :]), 0.0)
            for t in (ZE, Y, U, HH):
                last = pool.memset(t[:], 0.0)
            last.then_inc(s_ms, 1)
            pool.wait_ge(s_in["b1"], 16)
            src, dst = b1w, b1p
            for x, n in enumerate(range(18, 12, -1)):
                pool.tensor_tensor(dst[:, 0:n * C], src[:, C:(n + 1) * C], src[:, 0:n * C], ALU.add
                                   ).then_inc(s_b1, 1)
                pool.wait_ge(s_b1, x + 1)
                src, dst = dst, src
            pool.wait_ge(s_wh0, 4)
            for h in range(2):
                m = pool.tensor_tensor(B1l[:, :, h, :], b1s[:, 2 * h:2 * h + 11:2, :], r32(B1h[:, :, h, :]),
                                       ALU.subtract)
            m.then_inc(s_b1, 1)

            def q3_full(g):
                pool.wait_ge(s_q3h, g)
                pool.wait_ge(s_q3l, g)
                for p in range(2):
                    m = pool.tensor_tensor(g3(Q3f[:, p, :]), q3s[:, p, :].unsqueeze(1).to_broadcast([128, NG, C]),
                                           bc(gslice(D32, g), C), ALU.mult)
                m.then_inc(s_q3f, 1)

            def q3_low(g):
                pool.wait_ge(s_q3h, g + 1)
                pool.tensor_tensor(Q3l[:, :, :], Q3f[:, :, :], r32(Q3h[:, :, :]), ALU.subtract).then_inc(s_q3l, 1)

            def piece(g, k):
                if k < 3:
                    pool.wait_ge(s_q2h, 3 * g + k + 1)
                    pool.tensor_tensor(Q2l[:, k, :], Q2f[:, k, :], r32(Q2h[:, k, :]), ALU.subtract
                                       ).then_inc(s_q2l, 1)
                else:
                    pool.wait_ge(s_wh, 4 * g + k - 2)
                    v, d = k - 3, g % 2
                    a, h = g3(GT[:, v, :]), r32(Wh[:, d, v, :, 0, :])
                    pool.tensor_tensor(Wl[:, d, v, :, 0, :], a, h, ALU.subtract).then_inc(s_wl, 1)

            for k in range(3, 7):
                piece(0, k)
            q3_full(1)
            q3_low(1)
            pool.wait_ge(s_sc, SC_CV)
            for j in range(TR):
                pool.memset(T[0:64, j, :, 0:1], 0.0)
            for b in range(B):
                g, i = divmod(b, NG)
                if g + 1 < NGR:
                    for k in range(7):
                        if PIECE_SLOT[k] == i - 1:
                            piece(g + 1, k)
                if g + 2 < NGR:
                    if i == 3:
                        q3_full(g + 2)
                    if i == 5:
                        q3_low(g + 2)

        @block.vector
        def _(dve):
            chain = [0]

            def link(ins):
                chain[0] += 1
                ins.then_inc(s_ch, 1)
                dve.wait_ge(s_ch, chain[0])

            def reached(ins):
                ins.then_inc(s_sc, 1)

            tt = dve.tensor_tensor
            bias = lambda l: BB[:, 0, l:l + 1]

            def x_low(b):
                dve.wait_ge(s_xh, b + 1)
                if b >= 2:
                    dve.wait_ge(s_z, b - 1)
                dve.scalar_tensor_tensor(out=xl[:, b % 2, 0:K], in0=X[:, b // Q % XR, b % Q, :],
                                         scalar=S[:, 0, b:b + 1], in1=r32(xh[:, b % 2, 0:K]),
                                         op0=ALU.mult, op1=ALU.subtract).then_inc(s_xl, 1)

            def z_low(b):
                dve.wait_ge(s_zh, b + 1)
                if b >= 2:
                    dve.wait_ge(s_o, b - 1)
                dve.scalar_tensor_tensor(out=zl[:, b % 2, 1:513], in0=pz[b % 2][:, :],
                                         scalar=b0z[:, b:b + 1], in1=r32(zh[:, b % 2, 1:513]),
                                         op0=ALU.add, op1=ALU.subtract).then_inc(s_zl, 1)

            def piece(g, k):
                n = 7 * g + k
                dve.wait_ge(s_c, n + 1)
                src = g3(pc[n % 2][:, :])
                if k < 3:
                    if g:
                        dve.wait_ge(s_q2h, 3 * (g - 1) + k + 1)
                        dve.wait_ge(s_q2l, 3 * (g - 1) + k + 1)
                    tt(g3(Q2f[:, k, :]), src, bc(gslice(D21, g), C), ALU.mult).then_inc(s_ce, 1)
                else:
                    if g:
                        dve.wait_ge(s_wx, 4 * (g - 1) + k - 2)
                        dve.wait_ge(s_wl, 4 * (g - 1) + k - 2)
                    tt(g3(GT[:, k - 3, :]), src, bc(gslice(D10c, g), C), ALU.mult).then_inc(s_ce, 1)

            def cross(g, v):
                w = Wl[:, g % 2]
                dve.wait_ge(s_wl, 4 * g + v + 1)
                if v < 3:
                    dve.tensor_copy(w[0:64, v + 1, :, 1, :], r32(w[64:128, v, :, 0, :]))
                dve.tensor_copy(w[64:128, v, :, 1, :], r32(w[0:64, v, :, 0, :])).then_inc(s_wc, 1)

            def finish(n):
                dve.wait_ge(s_t, Q * (n + 1))
                dve.wait_ge(s_ed, 5 * (n * Q // EC) + 5)
                e = EP[:, n * Q:(n + 1) * Q, :]
                dve.tensor_copy(T[64:128, n % TR, :, 0:512:511], e[64:128])
                link(dve.tensor_copy(T[0:64, n % TR, :, 1:513:511], e[0:64]))
                tt(T[:, n % TR], T[:, n % TR], X[:, n % XR], ALU.add).then_inc(s_fin, 1)

            def finish_last(j):
                n = NQ - 1
                b = n * Q + j
                t = T[:, n % TR, j, :]
                dve.wait_ge(s_t, b + 1)
                dve.wait_ge(s_ed, 5 * (b // EC) + 5)
                dve.tensor_copy(t[64:128, 0:512:511], EP[64:128, b, :])
                link(dve.tensor_copy(t[0:64, 1:513:511], EP[0:64, b, :]))
                tt(t, t, X[:, n % XR, j, :], ALU.add).then_inc(s_fin, 1)

            def edge_in(c):
                cs = slice(c * EC, (c + 1) * EC)
                tt(XS[:], XE[:, cs, :], bc(S[:, 0, cs], 7), ALU.mult).then_inc(s_ed, 1)

            def edge(c, k):
                cs = slice(c * EC, (c + 1) * EC)
                dve.wait_ge(s_e, 4 * c + k + 1)
                lo, hi = slice(0, 64), slice(64, 128)
                if k == 0:
                    v = Y1[:, :, 0:5]
                    link(tt(v, pe_[:, 0:5 * EC].rearrange("p (b n) -> p b n", n=5), bc(b0z[:, cs], 5), ALU.add))
                    tt(ZE[lo, :, 1:6], v[lo], bc(D10[lo, cs], 5), ALU.mult)
                    tt(ZE[hi, :, 0:5], v[hi], bc(D10[hi, cs], 5), ALU.mult).then_inc(s_ed, 1)
                elif k == 1:
                    v = Y1[:, :, :]
                    tt(v[:, :, 0:5], pe_[:, 0:5 * EC].rearrange("p (b n) -> p b n", n=5),
                       bc(S[:, 1, cs], 5), ALU.mult)
                    link(tt(v[:, :, 5:9], pe_[:, 5 * EC:9 * EC].rearrange("p (b n) -> p b n", n=4),
                            bc(S[:, 1, cs], 4), ALU.mult))
                    for h, o in ((lo, 1), (hi, 0)):
                        dve.tensor_scalar(Y[h, :, o:o + 9:2], v[h, :, 0:5], BB[h, 0, 1:2], None, ALU.add)
                        m = dve.tensor_scalar(Y[h, :, o + 1:o + 8:2], v[h, :, 5:9], BB[h, 0, 1:2], None, ALU.add)
                    link(m)
                    link(tt(Y1[:, :, 0:9], Y[:, :, 1:10], Y[:, :, 0:9], ALU.add))
                    link(tt(Y2[:, :, 0:8], Y1[:, :, 1:9], Y1[:, :, 0:8], ALU.add))
                    link(tt(Y1[:, :, 0:7], Y2[:, :, 1:8], Y2[:, :, 0:7], ALU.add))
                    for h, o in ((lo, 1), (hi, 0)):
                        m = dve.scalar_tensor_tensor(out=U[h, :, o:o + 7], in0=Y1[h, :, 0:7], scalar=0.25,
                                                     in1=bc(S[h, 2, cs], 7), op0=ALU.mult, op1=ALU.mult)
                    m.then_inc(s_ed, 1)
                elif k == 2:
                    v = Y1[:, :, 0:6]
                    link(tt(v, pe_[:, 0:6 * EC].rearrange("p (b n) -> p b n", n=6), bc(DD[:, 2, cs], 6), ALU.mult))
                    for h, o in ((lo, 2), (hi, 0)):
                        m = dve.tensor_scalar(HH[h, :, o:o + 6], v[h], BB[h, 0, 2:3], None, ALU.add)
                    link(m)
                    link(tt(Y1[:, :, 0:7], HH[:, :, 1:8], HH[:, :, 0:7], ALU.add))
                    link(tt(Y2[:, :, 0:6], Y1[:, :, 1:7], Y1[:, :, 0:6], ALU.add))
                    link(tt(Y1[:, :, 0:5], Y2[:, :, 1:6], Y2[:, :, 0:5], ALU.add))
                    dve.scalar_tensor_tensor(out=XB[:], in0=Y1[:, :, 0:5], scalar=0.125, in1=bc(S[:, 3, cs], 5),
                                             op0=ALU.mult, op1=ALU.mult).then_inc(s_ed, 1)
                else:
                    v = Y1[:, :, 0:2]
                    link(tt(v, pe_[:, 0:2 * EC].rearrange("p (b n) -> p b n", n=2), bc(DD[:, 3, cs], 2), ALU.mult))
                    for h, n in ((lo, 0), (hi, 1)):
                        dve.tensor_scalar(EP[hi, cs, n:n + 1], v[h, :, 0:1], BB[h, 0, 3:4], None, ALU.add)
                        m = dve.tensor_scalar(EP[lo, cs, n:n + 1], v[h, :, 1:2], BB[h, 0, 3:4], None, ALU.add)
                    m.then_inc(s_ed, 1)

            def newton(l):
                link(tt(tmp[:, l], RR[:, l], RR[:, l], ALU.mult))
                link(tt(tmp[:, l], tmp[:, l], AA[:, l], ALU.mult))
                link(dve.tensor_scalar(tmp[:, l], tmp[:, l], -0.5, 1.5, ALU.mult, ALU.add))
                link(tt(DD[:, l], tmp[:, l], RR[:, l], ALU.mult))

            psv = ps[:, :].rearrange("p (l b) -> p l b", l=4)
            dve.wait_ge(s_in["wt"], 16)
            link(tt(SQ[:, 2], WT[:, 2], WT[:, 2], ALU.mult))
            link(tt(WSQ[:, 2, :], SQ[:, 2, 0], SQ[:, 2, 1], ALU.add))
            tt(WSQ[:, 2, :], WSQ[:, 2, :], SQ[:, 2, 2], ALU.add)
            dve.wait_ge(s_in["bb"], 16)
            dve.wait_ge(s_pp, 1)
            link(tt(S[:], psv, bc(BB[:, 1, :], B), ALU.add))
            reached(tt(tmp[:, 2], S[:, 2], S[:, 2], ALU.mult))
            tt(SQ[:, 0:2], WT[:, 0:2], WT[:, 0:2], ALU.mult)
            dve.wait_ge(s_pp, 2)
            reached(dve.tensor_scalar(AA[:, 2], psv[:, 2], EPS, None, ALU.add))
            dve.wait_ge(s_wh0, 2)
            tt(L0l[:], L0f[:], r32(L0h[:]), ALU.subtract)
            reached(tt(A2l[:], A2f[:], r32(A2h[:]), ALU.subtract))
            dve.wait_ge(s_sq, 1)
            link(dve.reciprocal(RR[:, 2], RR[:, 2]))
            newton(2)
            link(tt(D32[:], DD[:, 2], S[:, 3], ALU.mult))
            dve.wait_ge(s_in["q3"], 16)
            for p in range(2):
                m = tt(g3(Q3f[:, p, :]), q3s[:, p, :].unsqueeze(1).to_broadcast([128, NG, C]),
                       bc(gslice(D32, 0), C), ALU.mult)
            m.then_inc(s_q3f, 1)
            link(tt(SQ[:, 3], WT[:, 3], WT[:, 3], ALU.mult))
            tt(WSQ[:, 0:2], SQ[:, 0:2, 0], SQ[:, 0:2, 1], ALU.add)
            link(tt(WSQ[:, 3], SQ[:, 3, 0], SQ[:, 3, 1], ALU.add))
            dve.wait_ge(s_q3h, 1)
            tt(Q3l[:, :, :], Q3f[:, :, :], r32(Q3h[:, :, :]), ALU.subtract).then_inc(s_q3l, 1)
            tt(WSQ[:, 0:2], WSQ[:, 0:2], SQ[:, 0:2, 2], ALU.add)
            tt(WSQ[:, 3], WSQ[:, 3], SQ[:, 3, 2], ALU.add)
            tt(tmp[:, 0:2], S[:, 0:2], S[:, 0:2], ALU.mult)
            tt(D21[:], S[:, 1], S[:, 2], ALU.mult)
            reached(tt(tmp[:, 3], S[:, 3], S[:, 3], ALU.mult))
            x_low(0)
            dve.wait_ge(s_pp, 3)
            dve.tensor_scalar(AA[:, 0:2], psv[:, 0:2], EPS, None, ALU.add)
            reached(dve.tensor_scalar(AA[:, 3], psv[:, 3], EPS, None, ALU.add))

            def q2_low(k):
                dve.wait_ge(s_q2h, k + 1)
                tt(Q2l[:, k, :], Q2f[:, k, :], r32(Q2h[:, k, :]), ALU.subtract).then_inc(s_q2l, 1)

            dve.wait_ge(s_b1, 6)
            piece(0, 0)
            dve.wait_ge(s_sq, 2)
            dve.reciprocal(RR[:, 0:2], RR[:, 0:2])
            q2_low(0)
            piece(0, 1)
            link(dve.reciprocal(RR[:, 3], RR[:, 3]))
            q2_low(1)
            piece(0, 2)
            link(tt(tmp[:], RR, RR, ALU.mult))
            q2_low(2)
            link(tt(tmp[:], tmp[:], AA[:], ALU.mult))
            link(dve.tensor_scalar(tmp[:], tmp[:], -0.5, 1.5, ALU.mult, ALU.add))
            tt(DD[:, 0:2], tmp[:, 0:2], RR[:, 0:2], ALU.mult)
            link(tt(DD[:, 3], tmp[:, 3], RR[:, 3], ALU.mult))
            link(dve.scalar_tensor_tensor(out=D10c[:], in0=DD[:, 0], scalar=1.0 / 32.0, in1=DD[:, 1],
                                          op0=ALU.mult, op1=ALU.mult))
            link(tt(b0z[:], AA[:, 0], DD[:, 0], ALU.mult))
            reached(dve.tensor_scalar(b0z[:], b0z[:], bias(0), None, ALU.mult))
            link(tt(WSM[:], WT[:, 2:4, 0], WT[:, 2:4, 1], ALU.add))
            tt(WSM[:], WSM[:], WT[:, 2:4, 2], ALU.add)
            reached(dve.tensor_scalar(tmp[:, 0, :], S[:, 2, :], bias(1), 2.0, ALU.mult, ALU.mult))
            dve.wait_ge(s_ms, 1)
            z_low(0)
            x_low(1)
            piece(0, 3)
            dve.wait_ge(s_pp, 4)
            link(tt(hb[:], ps[:, 0:128], DD[:, 2, :], ALU.mult))
            link(dve.tensor_scalar(hb[:], hb[:], bias(2), None, ALU.add))
            reached(tt(tmp[:, 1, :], hb[:], S[:, 3, :], ALU.mult))
            piece(0, 4)
            cross(0, 0)
            piece(0, 5)
            cross(0, 1)
            dve.wait_ge(s_pp, 5)
            link(tt(cv[:], ps[:, 128:256], DD[:, 3, :], ALU.mult))
            reached(dve.tensor_scalar(cv[:], cv[:], bias(3), None, ALU.add))
            piece(0, 6)
            cross(0, 2)
            cross(0, 3)
            tt(D10[:], DD[:, 0], DD[:, 1], ALU.mult)
            dve.wait_ge(s_in["xe"], 16)
            edge_in(0)
            for b in range(B + 1):
                g, i = divmod(b, NG)
                if b + 2 < B:
                    x_low(b + 2)
                if b + 1 < B:
                    z_low(b + 1)
                if g + 1 < NGR:
                    for k in range(7):
                        if PIECE_SLOT[k] == i - 1:
                            piece(g + 1, k)
                    for k in range(3, 7):
                        if PIECE_SLOT[k] == i - 2:
                            cross(g + 1, k - 3)
                pg, pi = divmod(b - 1, NG)
                if (pg, pi) in groups_edge:
                    c, k = groups_edge[(pg, pi)]
                    edge(c, k)
                    if k == 3 and c + 1 < B // EC:
                        edge_in(c + 1)
                if b == 6:
                    finish(0)
                elif b > 6 and b % Q == 0 and b < B:
                    finish(b // Q - 1)
                if b > B - Q:
                    finish_last(b - 1 - (B - Q))



def layouts(x, cond_512, w, bia, mw, mb):
    import numpy as np
    f = np.float32
    B, C, L = x.shape
    xp = np.zeros((B, C, L + 2), f); xp[:, :, 1:L + 1] = x
    xin = np.ascontiguousarray(xp.reshape(B, C, L // 2 + 1, 2).transpose(0, 3, 1, 2)).reshape(B, 128, L // 2 + 1)
    xe = np.concatenate([xp[:, :, 0:7], xp[:, :, L - 5:L + 2]], axis=1).transpose(1, 0, 2)
    l0 = np.zeros((2, C, 2, 2, C), f)
    for j in range(2):
        for r in range(2):
            for h in range(2):
                t = 2 * j + r - h
                if 0 <= t < 3: l0[r, :, j, h, :] = w[0, :, :, t].T
    a2 = np.zeros((2, C, 4, C), f)
    for s in range(4):
        for r in range(2):
            if 0 <= s - r < 3: a2[r, :, s, :] = w[2, :, :, s - r]
    b1 = np.zeros((2, C, 19, C), f)
    for s in range(-8, 11):
        for r in range(2):
            if 0 <= s - r < 3: b1[r, :, s + 8, :] = w[1, :, :, 2 - (s - r)].T
    q3 = np.zeros((2, C, 2, C), f)
    for p in range(2):
        for r in range(2):
            if 2 * p + r < 3: q3[r, :, p, :] = w[3, :, :, 2 * p + r].T
    ed = np.zeros((2, C, 4, 3, 2, C), f)
    for s in range(2):
        ed[s, :, :, :, s, :] = w.transpose(2, 0, 3, 1)
        ed[s, :, 1, :, s, :] = w[1].transpose(0, 2, 1)
    wt = w.transpose(2, 0, 3, 1)
    wt = np.stack([wt, wt], axis=3)
    mwt = np.stack([mw.transpose(2, 0, 1)] * 2, axis=2)
    bb = np.stack([bia.T, mb.T], axis=1)
    bb = np.concatenate([bb, bb], axis=0)
    out = dict(xin=xin, xe=xe, l0=l0.reshape(128, 256), a2=a2.reshape(128, 256), b1=b1.reshape(128, 19 * 64),
               q3=q3.reshape(128, 128), ed=ed.reshape(128, 12 * 128), wt=wt.reshape(64, 12 * 128),
               mwt=mwt.reshape(128, 512), bb=bb.reshape(128, 8), st=cond_512.T)
    return {k: np.ascontiguousarray(v) for k, v in out.items()}


_ORDER = ["xin", "xe", "l0", "a2", "b1", "q3", "ed", "wt", "mwt", "bb", "st"]


def kernel(x, cond_512, L0_cond_weights, L0_cond_biases, L0_cond_mod_w, L0_cond_mod_b):
    import numpy as np
    import concourse.bacc as bacc
    from concourse.bass_utils import run_bass_kernel_spmd

    d = layouts(*(np.asarray(a) for a in (x, cond_512, L0_cond_weights, L0_cond_biases, L0_cond_mod_w,
                                          L0_cond_mod_b)))
    d["xe"] = d["xe"].reshape(128, B, 7)
    nc = bacc.Bacc("TRN2", target_bir_lowering=False, num_devices=1)
    arrays = {f"in_{n}": d[n] for n in _ORDER}
    args = [nc.dram_tensor(f"in_{n}", d[n].shape, F32, kind="ExternalInput").ap() for n in _ORDER]
    out = nc.dram_tensor("out_0", (B, 128, K), F32, kind="ExternalOutput").ap()
    build(nc, *args, out)
    r = run_bass_kernel_spmd(nc, [arrays], core_ids=[0])
    o = r.results[0]["out_0"].reshape(B, 2, C, K).transpose(0, 2, 3, 1).reshape(B, C, 2 * K)
    return np.ascontiguousarray(o[:, :, 1:2 * K - 1])
```

```python
from contextlib import ExitStack

import concourse.bass as bass
from concourse import mybir

ALU = mybir.AluOpType
ACT = mybir.ActivationFunctionType
F32 = mybir.dt.float32
F32R = mybir.dt.float32r

B = 128
C = 64
NG = 8
NGR = B // NG
Q = 2
NQ = B // Q
EC = 32
K = 513
XR = 5
TR = 3
XH = 3
EPS = 1e-8 * (C * 9)
STAGE_A = [[(0, 0)], [(0, 1), (1, 0)], [(1, 1)]]
STAGE_B = [[0, 1], [0, 1, 2], [0, 1, 2], [2]]
PIECE_SLOT = [0, 0, 1, 2, 2, 3, 4]


def build(nc, xin, xe, l0, a2, b1, q3, ed, wt, mwt, bb, st, out):
    with ExitStack() as ctx:
        def sb(name, shape, dt=F32):
            return ctx.enter_context(nc.sbuf_tensor(name, shape, dt))

        def sem(name):
            return ctx.enter_context(nc.semaphore(name))

        X = sb("X", [128, XR, Q, K])
        T = sb("T", [128, TR, Q, K])
        D = sb("D", [128, 2, 2, 256])
        xh = sb("xh", [128, XH, 768], F32R)
        xl = sb("xl", [128, XH, 768], F32R)
        M1 = sb("M1", [128, 2, 256])
        zf = sb("zf", [128, 512])
        zh = sb("zh", [128, 2, 516], F32R)
        zl = sb("zl", [128, 2, 516], F32R)
        Wh = sb("Wh", [128, 2, 4 * NG, 2, C], F32R)
        Wl = sb("Wl", [128, 2, 4 * NG, 2, C], F32R)
        GT = sb("GT", [128, 4, NG * C])
        Q2f = sb("Q2f", [128, 3, NG * C])
        Q2h = sb("Q2h", [128, 3, NG * C], F32R)
        Q2l = sb("Q2l", [128, 2, NG * C], F32R)
        Q3f = sb("Q3f", [128, 2, NG * C])
        Q3h = sb("Q3h", [128, 2, NG * C], F32R)
        Q3l = sb("Q3l", [128, 1, NG * C], F32R)
        L0h = sb("L0h", [128, 384], F32R)
        L0l = sb("L0l", [128, 384], F32R)
        A2h = sb("A2h", [128, 512], F32R)
        A2l = sb("A2l", [128, 512], F32R)
        B1h = sb("B1h", [128, 6, 2, C], F32R)
        B1l = sb("B1l", [128, 6, 2, C], F32R)
        B1dh = sb("B1dh", [128, 3, 2, C], F32R)
        B1dl = sb("B1dl", [128, 3, 2, C], F32R)
        q3s = sb("q3s", [128, 2, C])
        E = sb("E", [128, 4, 3, 128])
        MW = sb("MW", [128, 4, 128])
        ST = sb("ST", [128, B])
        BB = sb("BB", [128, 2, 4])
        S = sb("S", [128, 4, B])
        AA = sb("AA", [128, 4, B])
        DD = sb("DD", [128, 4, B])
        tmp = sb("tmp", [128, 4, B])
        D10 = sb("D10", [128, B])
        D10c = sb("D10c", [128, B])
        D21 = sb("D21", [128, B])
        D32 = sb("D32", [128, B])
        b0z = sb("b0z", [128, B])
        one = sb("one", [128, 1])
        cv = sb("cv", [128, B])
        XE = sb("XE", [128, B, 7])
        ZE = sb("ZE", [128, EC, 6])
        Y = sb("Y", [128, EC, 10])
        U = sb("U", [128, EC, 8])
        HH = sb("HH", [128, EC, 8])
        Tw = T[0:64].rearrange("p s q k -> p (s q k)")
        WT = Tw[:, 0:1536].rearrange("p (l t m) -> p l t m", l=4, t=3)
        SQ = Tw[:, 1536:3072].rearrange("p (l t m) -> p l t m", l=4, t=3)
        WSQ = X[0:64, XR - 1, 0, 0:512].rearrange("p (l m) -> p l m", l=4)
        WSM = X[0:64, XR - 1, 1, 0:256].rearrange("p (l m) -> p l m", l=2)
        hb = tmp[:, 2]
        edge_buf = lambda t, a, n: t[:].rearrange("p l b -> p (l b)")[:, a * EC:(a + n) * EC].rearrange(
            "p (b n) -> p b n", n=n)
        Y1, XS = edge_buf(AA, 0, 9), edge_buf(AA, 9, 7)
        EP = MW[:, 0:2].rearrange("p l b -> p (l b)").rearrange("p (b n) -> p b n", n=2)
        Y2, XB = edge_buf(tmp, 0, 8), edge_buf(tmp, 8, 5)
        b1s = GT[:, 0:3, :].rearrange("p v n -> p (v n)")[:, 0:14 * C].rearrange("p (s i) -> p s i", i=C)
        b1p = Q2f[:, :, :].rearrange("p v n -> p (v n)")
        RR = MW[:, :, :]
        b1w = GT[:, 0:3, :].rearrange("p v n -> p (v n)")
        L0f = GT[:, :, :].rearrange("p v n -> p (v n)")[:, 14 * C:20 * C]
        A2f = GT[:, :, :].rearrange("p v n -> p (v n)")[:, 20 * C:28 * C]
        def psum(name):
            return ctx.enter_context(nc.psum_tensor(name, [128, 512], F32))

        pz = [psum("pz0"), psum("pz1")]
        po = [psum("po0"), psum("po1")]
        pc = [psum("pc0"), psum("pc1")]
        pe_ = psum("pe")
        ps = psum("ps")
        pm = [ps[:, 0:256], ps[:, 256:512]]

        s_in = {n: sem("i_" + n) for n in ("mwt", "st", "bb", "wt", "q3", "a2", "l0", "b1", "ed", "xe")}
        s_x = [sem(f"x{i}") for i in range(XR)]
        s_st = [sem(f"st{i}") for i in range(TR)]
        s_wx, s_wc = sem("wx"), sem("wc")
        s_w = [sem("w0"), sem("w1")]
        s_xh, s_xl, s_zh, s_zl = sem("xh"), sem("xl"), sem("zh"), sem("zl")
        s_d = sem("d")
        s_m, s_m1, s_zf = sem("m"), sem("m1"), sem("zf")
        s_l0s, s_l0h = sem("l0s"), sem("l0h")
        s_z, s_o, s_t = sem("z"), sem("o"), sem("t")
        s_fin = sem("fin")
        s_c, s_ce = sem("c"), sem("ce")
        s_q3f, s_q3h, s_q3l = sem("q3f"), sem("q3h"), sem("q3l")
        s_q2h, s_q2l, s_wh, s_wl = sem("q2h"), sem("q2l"), sem("wh"), sem("wl")
        s_e, s_ed = sem("e"), sem("ed")
        s_pp, s_ch = sem("pp"), sem("ch")
        s_one = sem("one")
        s_ms = sem("ms")
        s_sq = sem("sq")
        s_sc, s_wh0 = sem("sc"), sem("wh0")
        s_b1 = sem("b1")

        SC_SQ2, SC_A2, SC_WL, SC_SQ, SC_B1D, SC_A, SC_D, SC_HB1, SC_HB2, SC_CV = range(1, 11)
        r32 = lambda ap: ap.bitcast(F32)

        def bc(ap, n):
            return ap.unsqueeze(2).to_broadcast([ap.shape[0], ap.shape[1], n])

        def split_mm(eng, o, wh_, wl_, rh, rl, first, last):
            eng.matmul(o, wh_, rh, start=first, stop=False)
            eng.matmul(o, wh_, rl, start=False, stop=False)
            return eng.matmul(o, wl_, rh, start=False, stop=last)

        def lone_mm(eng, o, wh_, wl_, r, first, last):
            eng.matmul(o, wh_, r, start=first, stop=False)
            return eng.matmul(o, wl_, r, start=False, stop=last)

        def lone_low(eng, h, f):
            return eng.tensor_tensor(h, f, r32(h), ALU.subtract)

        gslice = lambda ap, g: ap[:, g * NG:(g + 1) * NG]
        g3 = lambda ap: ap.rearrange("p (b o) -> p b o", b=NG)
        groups_edge = {}
        for k in range(4):
            groups_edge[(0, (0, 1, 2, 3)[k])] = (0, k)
        for c in range(1, B // EC):
            for k in range(4):
                groups_edge[(EC // NG * c - 1, 2 * k)] = (c, k)

        block = ctx.enter_context(nc.Block())

        @block.sync
        def _(sp):
            for n, dst, src in (("mwt", MW[:], mwt.rearrange("p (l m) -> p l m", l=4)),
                                ("bb", BB[:], bb.rearrange("p (k l) -> p k l", k=2)),
                                ("b1", b1w[:, 0:14 * C], b1),
                                ("q3", q3s[:], q3.rearrange("p (k o) -> p k o", k=2))):
                sp.dma_start(dst, src).then_inc(s_in[n], 16)

            def load(n):
                if n >= XR:
                    sp.wait_ge(s_fin, n - XR + 1)
                sp.dma_start(X[:, n % XR], xin[n * Q:(n + 1) * Q].rearrange("b p k -> p b k")
                             ).then_inc(s_x[n % XR], 16)

            def store(n):
                if n < NQ - 1:
                    sp.wait_ge(s_fin, n + 1)
                    sp.dma_start(out[n * Q:(n + 1) * Q].rearrange("b p k -> p b k"), T[:, n % TR]
                                 ).then_inc(s_st[n % TR], 16)
                    return
                for j in range(Q):
                    sp.wait_ge(s_fin, n + 1 + j)
                    sp.dma_start(out[n * Q + j], T[:, n % TR, j, :]).then_inc(s_st[n % TR], 16)

            def cross(g, v):
                sp.wait_ge(s_wh, 4 * g + v + 1)
                sp.wait_ge(s_wl, 4 * g + v + 1)
                for t in (Wh, Wl):
                    w = r32(t[:, g % 2])
                    a, b = slice(v * NG, v * NG + NG), slice(v * NG + NG, v * NG + 2 * NG)
                    sp.dma_start(w[64:128, a, 1, :], w[0:64, a, 0, :]).then_inc(s_w[g % 2], 16)
                    if v < 3:
                        sp.dma_start(w[0:64, b, 1, :], w[64:128, a, 0, :]).then_inc(s_w[g % 2], 16)

            load(0)
            sp.dma_start(XE[:], xe).then_inc(s_in["xe"], 16)
            for n in range(1, XR - 1):
                load(n)
            sp.wait_ge(s_sc, SC_CV)
            load(XR - 1)
            for n in range(NQ):
                g, i = divmod(n, NG // Q)
                for v in range(4):
                    if g + 1 < NGR and i == ((1, 1, 2, 2) if g else (0, 0, 2, 2))[v]:
                        cross(g + 1, v)
                store(n)
                if n + XR < NQ:
                    load(n + XR)
            for i in range(TR):
                sp.wait_ge(s_st[i], 16 * (len(range(i, NQ, TR)) + (Q - 1 if (NQ - 1) % TR == i else 0)))

        @block.tensor
        def _(pe):
            def conv_z(b):
                pe.wait_ge(s_xh, b + 1)
                pe.wait_ge(s_xl, b + 1)
                if b >= 1:
                    pe.wait_ge(s_m1, b)
                if b >= 2:
                    pe.wait_ge(s_zf, b - 1)
                h, l = xh[:, b % XH], xl[:, b % XH]
                o = pz[b % 2]
                split_mm(pe, pm[b % 2], L0h[:, 256:384], L0l[:, 256:384], h[:, 512:768], l[:, 512:768], True, True
                         ).then_inc(s_m, 1)
                for e in range(2):
                    c, d = slice(128 * e, 128 * e + 128), slice(256 * e, 256 * e + 256)
                    m = split_mm(pe, o[:, d], L0h[:, c], L0l[:, c], h[:, d], l[:, d], True, True)
                m.then_inc(s_z, 1)

            def conv_o(b):
                g, i = divmod(b, NG)
                if i == 0:
                    pe.wait_ge(s_wh, 4 * (g + 1))
                    pe.wait_ge(s_wl, 4 * (g + 1))
                    if g:
                        pe.wait_ge(s_w[g % 2], 14 * 16 * ((g + 1) // 2))
                    else:
                        pe.wait_ge(s_wx, 4)
                        pe.wait_ge(s_wc, 4)
                pe.wait_ge(s_zh, b + 1)
                pe.wait_ge(s_zl, b + 1)
                if b >= 2:
                    pe.wait_ge(s_t, b - 1)
                for j in range(4):
                    w = [t[:, g % 2, j * NG + i].rearrange("p r o -> p (r o)") for t in (Wh, Wl)]
                    m = split_mm(pe, po[b % 2][:, :], w[0], w[1], zh[:, b % 2, j:j + 512], zl[:, b % 2, j:j + 512],
                                 j == 0, j == 3)
                m.then_inc(s_o, 1)

            def piece(g, k):
                n = 7 * g + k
                o = pc[n % 2][:, :]
                if n >= 2:
                    pe.wait_ge(s_ce, n - 1)
                if k == 0:
                    pe.wait_ge(s_q3h, 2 * g + 2)
                    pe.wait_ge(s_q3l, 2 * g + 1)
                if k == 1:
                    pe.wait_ge(s_q3l, 2 * g + 2)
                if k < 3:
                    prods = STAGE_A[k]
                    for x, (p, d) in enumerate(prods):
                        c0 = 128 * d + 256 * p
                        w = A2h[:, c0:c0 + 128], A2l[:, c0:c0 + 128]
                        if p == 0:
                            m = split_mm(pe, o, *w, Q3h[:, 0, :], Q3l[:, 0, :], x == 0, x == len(prods) - 1)
                        else:
                            m = lone_mm(pe, o, *w, Q3h[:, 1, :], x == 0, x == len(prods) - 1)
                else:
                    v = k - 3
                    need = 3 * g + STAGE_B[v][-1] + 1
                    pe.wait_ge(s_q2h, need)
                    pe.wait_ge(s_q2l, need)
                    for x, p in enumerate(STAGE_B[v]):
                        first, last = x == 0, x == len(STAGE_B[v]) - 1
                        if p < 2:
                            w = [t[:, 2 * v - p + 1].rearrange("p r i -> p (r i)") for t in (B1h, B1l)]
                            m = split_mm(pe, o, *w, Q2h[:, p, :], Q2l[:, p, :], first, last)
                        else:
                            w = [t[:, v - 1].rearrange("p r i -> p (r i)") for t in (B1dh, B1dl)]
                            m = lone_mm(pe, o, *w, Q2h[:, 2, :], first, last)
                m.then_inc(s_c, 1)

            def edge(c, k):
                pe.wait_ge(s_ed, 5 * c + k + 1)
                if k == 0:
                    for t in range(3):
                        m = pe.matmul(pe_[:, 0:5 * EC], E[:, 0, t, :], XS[:, :, t:t + 5], start=t == 0, stop=t == 2)
                elif k == 1:
                    pe.matmul(pe_[:, 0:5 * EC], E[:, 1, 0, :], ZE[:, :, 1:6], start=True, stop=False)
                    pe.matmul(pe_[:, 0:5 * EC], E[:, 1, 2, :], ZE[:, :, 0:5], start=False, stop=True)
                    m = pe.matmul(pe_[:, 5 * EC:9 * EC], E[:, 1, 1, :], ZE[:, :, 1:5], start=True, stop=True)
                elif k == 2:
                    for t in range(3):
                        m = pe.matmul(pe_[:, 0:6 * EC], E[:, 2, t, :], U[:, :, t:t + 6], start=t == 0, stop=t == 2)
                else:
                    for t in range(3):
                        m = pe.matmul(pe_[:, 0:2 * EC], E[:, 3, t, :], XB[:, :, t:t + 3:2], start=t == 0, stop=t == 2)
                m.then_inc(s_e, 1)

            for n in ("mwt", "st"):
                pe.wait_ge(s_in[n], 16)
            for l in range(4):
                m = pe.matmul(ps[:, l * 128:l * 128 + 128], MW[:, l, :], ST[:, :], start=True, stop=True)
            m.then_inc(s_pp, 1)
            pe.wait_ge(s_sc, SC_SQ2)
            pe.matmul(ps[:, 256:384], WSQ[:, 2, :], tmp[0:64, 2, :], start=True, stop=True).then_inc(s_pp, 1)
            pe.wait_ge(s_sc, SC_WL)
            piece(0, 0)
            pe.wait_ge(s_sc, SC_SQ)
            for l in (0, 1, 3):
                m = pe.matmul(ps[:, l * 128:l * 128 + 128], WSQ[:, l, :], tmp[0:64, l, :], start=True, stop=True)
            m.then_inc(s_pp, 1)
            piece(0, 1)
            piece(0, 2)
            pe.wait_ge(s_b1, 7)
            piece(0, 3)
            pe.wait_ge(s_sc, SC_B1D)
            piece(0, 4)
            piece(0, 5)
            pe.wait_ge(s_sc, SC_A)
            conv_z(0)
            piece(0, 6)
            conv_z(1)
            pe.wait_ge(s_sc, SC_HB1)
            pe.matmul(pe_[:, 0:128], WSM[:, 0, :], tmp[0:64, 0, :], start=True, stop=True).then_inc(s_pp, 1)
            conv_o(0)
            pe.wait_ge(s_sc, SC_HB2)
            pe.matmul(pe_[:, 128:256], WSM[:, 1, :], tmp[0:64, 1, :], start=True, stop=True).then_inc(s_pp, 1)
            pe.wait_ge(s_in["ed"], 16)
            for b in range(B):
                g, i = divmod(b, NG)
                if b + 2 < B:
                    conv_z(b + 2)
                if b:
                    conv_o(b)
                if g + 1 < NGR:
                    for k in range(7):
                        if PIECE_SLOT[k] == i:
                            piece(g + 1, k)
                if (g, i) in groups_edge:
                    edge(*groups_edge[(g, i)])

        @block.scalar
        def _(act):
            for n, dst, src in (("st", ST[:], st),
                                ("wt", WT, wt.rearrange("p (l t m) -> p l t m", l=4, t=3)),
                                ("a2", A2f, a2), ("l0", L0f[:, 0:256], l0),
                                ("ed", E[:], ed.rearrange("p (l t m) -> p l t m", l=4, t=3))):
                act.dma_start(dst, src).then_inc(s_in[n], 16)

            def x_high(b):
                n = b // Q
                if b % Q == 0:
                    act.wait_ge(s_x[n % XR], 16 * (n // XR + 1))
                if b >= XH:
                    act.wait_ge(s_z, b - XH + 1)
                sc = S[:, 0, b:b + 1]
                act.activation(xh[:, b % XH, 512:768], X[:, n % XR, b % Q, 1:512:2], ACT.Identity, scale=sc)
                act.wait_ge(s_d, b + 1)
                act.activation(xh[:, b % XH, 0:512], D[:, b % 2].rearrange("p e m -> p (e m)"), ACT.Identity,
                               scale=sc).then_inc(s_xh, 1)

            def z_common(b):
                act.wait_ge(s_m, b + 1)
                if b >= 2:
                    act.wait_ge(s_zf, b - 1)
                act.activation(M1[:, b % 2], pm[b % 2], ACT.Identity, bias=b0z[:, b:b + 1]).then_inc(s_m1, 1)

            def z_high(b):
                act.wait_ge(s_zf, b + 1)
                if b >= 2:
                    act.wait_ge(s_o, b - 1)
                act.copy(zh[:, b % 2, 1:513], zf[:]).then_inc(s_zh, 1)

            def t_out(b):
                n = b // Q
                act.wait_ge(s_o, b + 1)
                if b % Q == 0 and n >= TR:
                    act.wait_ge(s_st[n % TR], 16 * (n // TR))
                act.activation(T[:, n % TR, b % Q, 1:K], po[b % 2][:, :], ACT.Identity,
                               bias=cv[:, b:b + 1], scale=DD[:, 3, b:b + 1]).then_inc(s_t, 1)

            def q3_high(g):
                for p in range(2):
                    act.wait_ge(s_q3f, 2 * g + p + 1)
                    if g:
                        act.wait_ge(s_c, 7 * (g - 1) + 3)
                    act.copy(Q3h[:, p, :], Q3f[:, p, :]).then_inc(s_q3h, 1)

            def piece(g, k):
                act.wait_ge(s_ce, 7 * g + k + 1)
                if k < 3:
                    if g:
                        act.wait_ge(s_c, 7 * g)
                    act.copy(Q2h[:, k, :], Q2f[:, k, :]).then_inc(s_q2h, 1)
                else:
                    if g >= 2 and k == 3:
                        act.wait_ge(s_o, NG * (g - 1))
                    v, w = k - 3, Wh[:, g % 2]
                    act.copy(w[:, v * NG:(v + 1) * NG, 0, :], g3(GT[:, v, :])).then_inc(s_wh, 1)

            def cross(v):
                w = lambda p, u, r: Wh[p, 0, u * NG:(u + 1) * NG, r, :]
                if v < 3:
                    act.copy(w(slice(0, 64), v + 1, 1), g3(GT[64:128, v, :]))
                act.copy(w(slice(64, 128), v, 1), g3(GT[0:64, v, :])).then_inc(s_wx, 1)

            act.wait_ge(s_one, 1)
            act.activation(one[:], one[:], ACT.Sqrt)
            act.wait_ge(s_in["wt"], 16)
            act.activation(SQ[:, 0:2], WT[:, 0:2], ACT.Square)
            act.activation(SQ[:, 3], WT[:, 3], ACT.Square).then_inc(s_sq, 1)
            act.wait_ge(s_in["a2"], 16)
            act.copy(A2h[:], A2f).then_inc(s_wh0, 1)
            act.wait_ge(s_in["l0"], 16)
            act.copy(L0h[:, 0:256], L0f[:, 0:256]).then_inc(s_wh0, 1)
            act.wait_ge(s_sc, SC_A2)
            act.activation(RR[:, 2, :], AA[:, 2, :], ACT.Sqrt).then_inc(s_sq, 1)
            q3_high(0)
            act.wait_ge(s_b1, 6)
            for h in range(2):
                act.copy(B1h[:, :, h, :], b1s[:, 2 * h:2 * h + 11:2, :]).then_inc(s_wh0, 1)
            for h in range(2):
                for r in range(2):
                    a = 2 + 2 * h + r
                    act.copy(B1dh[64 * r:64 * r + 64, :, h, :], b1s[64 * r:64 * r + 64, a:a + 9:4, :]
                             ).then_inc(s_wh0, 1)
            piece(0, 0)
            act.wait_ge(s_sc, SC_A)
            act.activation(RR[:, 0:2, :], AA[:, 0:2, :], ACT.Sqrt)
            act.activation(RR[:, 3, :], AA[:, 3, :], ACT.Sqrt).then_inc(s_sq, 1)
            act.wait_ge(s_l0s, 1)
            act.copy(L0h[:, 256:384], L0f[:, 256:384]).then_inc(s_l0h, 1)
            piece(0, 1)
            piece(0, 2)
            x_high(0)
            piece(0, 3)
            piece(0, 4)
            cross(0)
            x_high(1)
            piece(0, 5)
            cross(1)
            act.wait_ge(s_sc, SC_D)
            z_common(0)
            piece(0, 6)
            cross(2)
            act.wait_ge(s_ms, 1)
            z_high(0)
            cross(3)
            z_common(1)
            z_high(1)
            x_high(2)
            q3_high(1)
            x_high(3)
            for b in range(B):
                g, i = divmod(b, NG)
                if b == 0:
                    act.wait_ge(s_sc, SC_CV)
                    t_out(0)
                elif b + 1 < B:
                    z_high(b + 1)
                if b + 2 < B:
                    z_common(b + 2)
                if b + 4 < B:
                    x_high(b + 4)
                if g + 1 < NGR:
                    for k in range(7):
                        if PIECE_SLOT[k] == i - 1:
                            piece(g + 1, k)
                if b:
                    t_out(b)
                if i == 5 and g + 2 < NGR:
                    q3_high(g + 2)

        @block.gpsimd
        def _(pool):
            pool.memset(one[:], 1.0).then_inc(s_one, 1)
            for t in (zh, zl):
                pool.memset(r32(t[:, :, 0:1]), 0.0)
                pool.memset(r32(t[:, :, 513:516]), 0.0)
            for d in range(2):
                pool.memset(r32(Wh[0:64, d, 0:NG, 1, :]), 0.0)
                pool.memset(r32(Wl[0:64, d, 0:NG, 1, :]), 0.0)
            pool.memset(b1p[:, 0:14 * C], 0.0)
            for t in (ZE, Y, U, HH):
                last = pool.memset(t[:], 0.0)
            last.then_inc(s_ms, 1)
            pool.wait_ge(s_ms, 1)
            pool.wait_ge(s_in["b1"], 16)
            src, dst = b1w, b1p
            for n in range(1, 7):
                a, e = 2 * C, (6 + n) * C
                pool.tensor_tensor(dst[:, a:e], src[:, a:e], src[:, a - C:e - C], ALU.add).then_inc(s_b1, 1)
                pool.wait_ge(s_b1, n)
                src, dst = dst, src

            made = [0]

            def differences(b):
                n = b // Q
                if b % Q == 0:
                    pool.wait_ge(s_x[n % XR], 16 * (n // XR + 1))
                if b >= 2:
                    pool.wait_ge(s_xl, b - 1)
                x = X[:, n % XR, b % Q, :]
                pool.tensor_tensor(D[:, b % 2, 0, :], x[:, 0:511:2], x[:, 1:512:2], ALU.subtract)
                pool.tensor_tensor(D[:, b % 2, 1, :], x[:, 2:513:2], x[:, 1:512:2], ALU.subtract).then_inc(s_d, 1)
                made[0] += 1

            differences(0)
            pool.wait_ge(s_wh0, 4)
            for h in range(2):
                m = pool.tensor_tensor(B1l[:, :, h, :], b1s[:, 2 * h:2 * h + 11:2, :], r32(B1h[:, :, h, :]),
                                       ALU.subtract)
            m.then_inc(s_b1, 1)

            def q3_full(g):
                pool.wait_ge(s_q3h, 2 * g)
                pool.wait_ge(s_q3l, 2 * g)
                for p in range(2):
                    m = pool.tensor_tensor(g3(Q3f[:, p, :]), q3s[:, p, :].unsqueeze(1).to_broadcast([128, NG, C]),
                                           bc(gslice(D32, g), C), ALU.mult)
                    m.then_inc(s_q3f, 1)

            def q3_low(g):
                pool.wait_ge(s_q3h, 2 * g + 2)
                pool.tensor_tensor(Q3l[:, 0, :], Q3f[:, 0, :], r32(Q3h[:, 0, :]), ALU.subtract).then_inc(s_q3l, 1)
                pool.wait_ge(s_q3l, 2 * g + 1)
                pool.wait_ge(s_d, made[0])
                lone_low(pool, Q3h[64:128, 1, :], Q3f[64:128, 1, :]).then_inc(s_q3l, 1)
                pool.wait_ge(s_q3l, 2 * g + 2)

            def piece(g, k):
                if k < 3:
                    pool.wait_ge(s_q2h, 3 * g + k + 1)
                    if k < 2:
                        pool.tensor_tensor(Q2l[:, k, :], Q2f[:, k, :], r32(Q2h[:, k, :]), ALU.subtract
                                           ).then_inc(s_q2l, 1)
                    else:
                        pool.wait_ge(s_q2l, 3 * g + 2)
                        pool.wait_ge(s_d, made[0])
                        lone_low(pool, Q2h[64:128, 2, :], Q2f[64:128, 2, :]).then_inc(s_q2l, 1)
                        pool.wait_ge(s_q2l, 3 * g + 3)
                else:
                    pool.wait_ge(s_wh, 4 * g + k - 2)
                    v, d = k - 3, g % 2
                    a, w = g3(GT[:, v, :]), slice(v * NG, (v + 1) * NG)
                    pool.tensor_tensor(Wl[:, d, w, 0, :], a, r32(Wh[:, d, w, 0, :]), ALU.subtract).then_inc(s_wl, 1)

            for k in range(3):
                piece(0, k)
            differences(1)
            for k in range(3, 7):
                piece(0, k)
            differences(2)
            q3_full(1)
            q3_low(1)
            differences(3)
            differences(4)
            pool.wait_ge(s_sc, SC_CV)
            for j in range(TR):
                pool.memset(T[0:64, j, :, 0:1], 0.0)
            for b in range(B):
                g, i = divmod(b, NG)
                if b + 5 < B:
                    differences(b + 5)
                if g + 1 < NGR:
                    for k in range(7):
                        if PIECE_SLOT[k] == i - 1:
                            piece(g + 1, k)
                if g + 2 < NGR:
                    if i == 3:
                        q3_full(g + 2)
                    if i == 5:
                        q3_low(g + 2)

        @block.vector
        def _(dve):
            chain = [0]

            def link(ins):
                chain[0] += 1
                ins.then_inc(s_ch, 1)
                dve.wait_ge(s_ch, chain[0])

            def reached(ins):
                ins.then_inc(s_sc, 1)

            tt = dve.tensor_tensor
            bias = lambda l: BB[:, 0, l:l + 1]

            def x_low(b):
                dve.wait_ge(s_xh, b + 1)
                if b >= XH:
                    dve.wait_ge(s_z, b - XH + 1)
                sc = S[:, 0, b:b + 1]
                dve.scalar_tensor_tensor(out=xl[:, b % XH, 512:768], in0=X[:, b // Q % XR, b % Q, 1:512:2],
                                         scalar=sc, in1=r32(xh[:, b % XH, 512:768]),
                                         op0=ALU.mult, op1=ALU.subtract)
                dve.scalar_tensor_tensor(out=xl[:, b % XH, 0:512], in0=D[:, b % 2].rearrange("p e m -> p (e m)"),
                                         scalar=sc, in1=r32(xh[:, b % XH, 0:512]),
                                         op0=ALU.mult, op1=ALU.subtract).then_inc(s_xl, 1)

            def z_full(b):
                dve.wait_ge(s_z, b + 1)
                dve.wait_ge(s_m1, b + 1)
                if b >= 1:
                    dve.wait_ge(s_zh, b)
                    dve.wait_ge(s_zl, b)
                tt(zf[:].rearrange("p (m e) -> p m e", e=2), pz[b % 2][:, :].rearrange("p (e m) -> p m e", e=2),
                   bc(M1[:, b % 2], 2), ALU.add).then_inc(s_zf, 1)

            def z_low(b):
                dve.wait_ge(s_zh, b + 1)
                if b >= 2:
                    dve.wait_ge(s_o, b - 1)
                tt(zl[:, b % 2, 1:513], zf[:], r32(zh[:, b % 2, 1:513]), ALU.subtract).then_inc(s_zl, 1)

            def piece(g, k):
                n = 7 * g + k
                dve.wait_ge(s_c, n + 1)
                src = g3(pc[n % 2][:, :])
                if k < 3:
                    if g:
                        dve.wait_ge(s_q2h, 3 * (g - 1) + k + 1)
                        dve.wait_ge(s_q2l, 3 * (g - 1) + k + 1)
                    tt(g3(Q2f[:, k, :]), src, bc(gslice(D21, g), C), ALU.mult).then_inc(s_ce, 1)
                else:
                    if g:
                        dve.wait_ge(s_wh, 4 * (g - 1) + k - 2)
                        dve.wait_ge(s_wl, 4 * (g - 1) + k - 2)
                    tt(g3(GT[:, k - 3, :]), src, bc(gslice(D10c, g), C), ALU.mult).then_inc(s_ce, 1)

            def cross(v):
                w = lambda p, u, r: Wl[p, 0, u * NG:(u + 1) * NG, r, :]
                lo, hi = slice(0, 64), slice(64, 128)
                dve.wait_ge(s_wl, v + 1)
                if v < 3:
                    dve.tensor_copy(w(lo, v + 1, 1), r32(w(hi, v, 0)))
                dve.tensor_copy(w(hi, v, 1), r32(w(lo, v, 0))).then_inc(s_wc, 1)

            def finish(n):
                dve.wait_ge(s_t, Q * (n + 1))
                dve.wait_ge(s_ed, 5 * (n * Q // EC) + 5)
                e = EP[:, n * Q:(n + 1) * Q, :]
                dve.tensor_copy(T[64:128, n % TR, :, 0:512:511], e[64:128])
                link(dve.tensor_copy(T[0:64, n % TR, :, 1:513:511], e[0:64]))
                tt(T[:, n % TR], T[:, n % TR], X[:, n % XR], ALU.add).then_inc(s_fin, 1)

            def finish_last(j):
                n = NQ - 1
                b = n * Q + j
                t = T[:, n % TR, j, :]
                dve.wait_ge(s_t, b + 1)
                dve.wait_ge(s_ed, 5 * (b // EC) + 5)
                dve.tensor_copy(t[64:128, 0:512:511], EP[64:128, b, :])
                link(dve.tensor_copy(t[0:64, 1:513:511], EP[0:64, b, :]))
                tt(t, t, X[:, n % XR, j, :], ALU.add).then_inc(s_fin, 1)

            def edge_in(c):
                cs = slice(c * EC, (c + 1) * EC)
                tt(XS[:], XE[:, cs, :], bc(S[:, 0, cs], 7), ALU.mult).then_inc(s_ed, 1)

            def edge(c, k):
                cs = slice(c * EC, (c + 1) * EC)
                dve.wait_ge(s_e, 4 * c + k + 1)
                lo, hi = slice(0, 64), slice(64, 128)
                if k == 0:
                    v = Y1[:, :, 0:5]
                    link(tt(v, pe_[:, 0:5 * EC].rearrange("p (b n) -> p b n", n=5), bc(b0z[:, cs], 5), ALU.add))
                    tt(ZE[lo, :, 1:6], v[lo], bc(D10[lo, cs], 5), ALU.mult)
                    tt(ZE[hi, :, 0:5], v[hi], bc(D10[hi, cs], 5), ALU.mult).then_inc(s_ed, 1)
                elif k == 1:
                    v = Y1[:, :, :]
                    tt(v[:, :, 0:5], pe_[:, 0:5 * EC].rearrange("p (b n) -> p b n", n=5),
                       bc(S[:, 1, cs], 5), ALU.mult)
                    link(tt(v[:, :, 5:9], pe_[:, 5 * EC:9 * EC].rearrange("p (b n) -> p b n", n=4),
                            bc(S[:, 1, cs], 4), ALU.mult))
                    for h, o in ((lo, 1), (hi, 0)):
                        dve.tensor_scalar(Y[h, :, o:o + 9:2], v[h, :, 0:5], BB[h, 0, 1:2], None, ALU.add)
                        m = dve.tensor_scalar(Y[h, :, o + 1:o + 8:2], v[h, :, 5:9], BB[h, 0, 1:2], None, ALU.add)
                    link(m)
                    link(tt(Y1[:, :, 0:9], Y[:, :, 1:10], Y[:, :, 0:9], ALU.add))
                    link(tt(Y2[:, :, 0:8], Y1[:, :, 1:9], Y1[:, :, 0:8], ALU.add))
                    link(tt(Y1[:, :, 0:7], Y2[:, :, 1:8], Y2[:, :, 0:7], ALU.add))
                    for h, o in ((lo, 1), (hi, 0)):
                        m = dve.scalar_tensor_tensor(out=U[h, :, o:o + 7], in0=Y1[h, :, 0:7], scalar=0.25,
                                                     in1=bc(S[h, 2, cs], 7), op0=ALU.mult, op1=ALU.mult)
                    m.then_inc(s_ed, 1)
                elif k == 2:
                    v = Y1[:, :, 0:6]
                    link(tt(v, pe_[:, 0:6 * EC].rearrange("p (b n) -> p b n", n=6), bc(DD[:, 2, cs], 6), ALU.mult))
                    for h, o in ((lo, 2), (hi, 0)):
                        m = dve.tensor_scalar(HH[h, :, o:o + 6], v[h], BB[h, 0, 2:3], None, ALU.add)
                    link(m)
                    link(tt(Y1[:, :, 0:7], HH[:, :, 1:8], HH[:, :, 0:7], ALU.add))
                    link(tt(Y2[:, :, 0:6], Y1[:, :, 1:7], Y1[:, :, 0:6], ALU.add))
                    link(tt(Y1[:, :, 0:5], Y2[:, :, 1:6], Y2[:, :, 0:5], ALU.add))
                    dve.scalar_tensor_tensor(out=XB[:], in0=Y1[:, :, 0:5], scalar=0.125, in1=bc(S[:, 3, cs], 5),
                                             op0=ALU.mult, op1=ALU.mult).then_inc(s_ed, 1)
                else:
                    v = Y1[:, :, 0:2]
                    link(tt(v, pe_[:, 0:2 * EC].rearrange("p (b n) -> p b n", n=2), bc(DD[:, 3, cs], 2), ALU.mult))
                    for h, n in ((lo, 0), (hi, 1)):
                        dve.tensor_scalar(EP[hi, cs, n:n + 1], v[h, :, 0:1], BB[h, 0, 3:4], None, ALU.add)
                        m = dve.tensor_scalar(EP[lo, cs, n:n + 1], v[h, :, 1:2], BB[h, 0, 3:4], None, ALU.add)
                    m.then_inc(s_ed, 1)

            def newton(l):
                link(tt(tmp[:, l], RR[:, l], RR[:, l], ALU.mult))
                link(tt(tmp[:, l], tmp[:, l], AA[:, l], ALU.mult))
                link(dve.tensor_scalar(tmp[:, l], tmp[:, l], -0.5, 1.5, ALU.mult, ALU.add))
                link(tt(DD[:, l], tmp[:, l], RR[:, l], ALU.mult))

            psv = ps[:, :].rearrange("p (l b) -> p l b", l=4)
            dve.wait_ge(s_in["wt"], 16)
            link(tt(SQ[:, 2], WT[:, 2], WT[:, 2], ALU.mult))
            link(tt(WSQ[:, 2, :], SQ[:, 2, 0], SQ[:, 2, 1], ALU.add))
            tt(WSQ[:, 2, :], WSQ[:, 2, :], SQ[:, 2, 2], ALU.add)
            dve.wait_ge(s_in["bb"], 16)
            dve.wait_ge(s_pp, 1)
            link(tt(S[:], psv, bc(BB[:, 1, :], B), ALU.add))
            reached(tt(tmp[:, 2], S[:, 2], S[:, 2], ALU.mult))
            tt(tmp[:, 0:2], S[:, 0:2], S[:, 0:2], ALU.mult)
            tt(tmp[:, 3], S[:, 3], S[:, 3], ALU.mult)
            dve.wait_ge(s_pp, 2)
            reached(dve.tensor_scalar(AA[:, 2], psv[:, 2], EPS, None, ALU.add))
            dve.wait_ge(s_wh0, 1)
            reached(tt(A2l[:], A2f, r32(A2h[:]), ALU.subtract))
            dve.wait_ge(s_sq, 2)
            link(dve.reciprocal(RR[:, 2], RR[:, 2]))
            newton(slice(2, 3))
            link(tt(D32[:], DD[:, 2], S[:, 3], ALU.mult))
            dve.wait_ge(s_in["q3"], 16)
            for p in range(2):
                tt(g3(Q3f[:, p, :]), q3s[:, p, :].unsqueeze(1).to_broadcast([128, NG, C]),
                   bc(gslice(D32, 0), C), ALU.mult).then_inc(s_q3f, 1)
            dve.wait_ge(s_sq, 1)
            tt(WSQ[:, 0:2], SQ[:, 0:2, 0], SQ[:, 0:2, 1], ALU.add)
            link(tt(WSQ[:, 3], SQ[:, 3, 0], SQ[:, 3, 1], ALU.add))
            dve.wait_ge(s_q3h, 1)
            tt(Q3l[:, 0, :], Q3f[:, 0, :], r32(Q3h[:, 0, :]), ALU.subtract).then_inc(s_q3l, 1)
            dve.wait_ge(s_q3h, 2)
            lone_low(dve, Q3h[64:128, 1, :], Q3f[64:128, 1, :]).then_inc(s_q3l, 1)
            tt(WSQ[:, 0:2], WSQ[:, 0:2], SQ[:, 0:2, 2], ALU.add)
            reached(tt(WSQ[:, 3], WSQ[:, 3], SQ[:, 3, 2], ALU.add))
            link(tt(D21[:], S[:, 1], S[:, 2], ALU.mult))
            dve.wait_ge(s_b1, 6)
            piece(0, 0)
            dve.wait_ge(s_wh0, 8)
            for h in range(2):
                for r in range(2):
                    a, t = 2 + 2 * h + r, slice(64 * r, 64 * r + 64)
                    m = tt(B1dl[t, :, h, :], b1s[t, a:a + 9:4, :], r32(B1dh[t, :, h, :]), ALU.subtract)
            reached(m)
            dve.wait_ge(s_pp, 3)
            dve.tensor_scalar(AA[:, 0:2], psv[:, 0:2], EPS, None, ALU.add)
            reached(dve.tensor_scalar(AA[:, 3], psv[:, 3], EPS, None, ALU.add))
            tt(L0f[:, 256:384], L0f[:, 0:128], L0f[:, 128:256], ALU.add).then_inc(s_l0s, 1)
            tt(L0l[:, 0:256], L0f[:, 0:256], r32(L0h[:, 0:256]), ALU.subtract)
            piece(0, 1)
            piece(0, 2)
            dve.wait_ge(s_sq, 3)
            link(dve.reciprocal(RR[:, 0:2], RR[:, 0:2]))
            link(tt(tmp[:, 0:2], RR[:, 0:2], RR[:, 0:2], ALU.mult))
            link(tt(tmp[:, 0:2], tmp[:, 0:2], AA[:, 0:2], ALU.mult))
            link(dve.tensor_scalar(tmp[:, 0:2], tmp[:, 0:2], -0.5, 1.5, ALU.mult, ALU.add))
            link(tt(DD[:, 0:2], tmp[:, 0:2], RR[:, 0:2], ALU.mult))
            link(dve.scalar_tensor_tensor(out=D10c[:], in0=DD[:, 0], scalar=1.0 / 32.0, in1=DD[:, 1],
                                          op0=ALU.mult, op1=ALU.mult))
            piece(0, 3)
            link(tt(b0z[:], AA[:, 0], DD[:, 0], ALU.mult))
            reached(dve.tensor_scalar(b0z[:], b0z[:], bias(0), None, ALU.mult))
            piece(0, 4)
            dve.wait_ge(s_l0h, 1)
            tt(L0l[:, 256:384], L0f[:, 256:384], r32(L0h[:, 256:384]), ALU.subtract)
            x_low(0)
            dve.wait_ge(s_xl, 1)
            piece(0, 5)
            cross(0)
            x_low(1)
            z_full(0)
            piece(0, 6)
            cross(1)
            link(tt(WSM, WT[:, 2:4, 0], WT[:, 2:4, 1], ALU.add))
            tt(WSM, WSM, WT[:, 2:4, 2], ALU.add)
            reached(dve.tensor_scalar(tmp[:, 0, :], S[:, 2, :], bias(1), 2.0, ALU.mult, ALU.mult))
            cross(2)
            dve.wait_ge(s_ms, 1)
            z_low(0)
            cross(3)
            z_full(1)
            dve.wait_ge(s_pp, 4)
            link(tt(hb, pe_[:, 0:128], DD[:, 2, :], ALU.mult))
            link(dve.tensor_scalar(hb, hb, bias(2), None, ALU.add))
            reached(tt(tmp[:, 1, :], hb, S[:, 3, :], ALU.mult))
            z_low(1)
            x_low(2)
            link(dve.reciprocal(RR[:, 3], RR[:, 3]))
            newton(slice(3, 4))
            dve.wait_ge(s_pp, 5)
            link(tt(cv[:], pe_[:, 128:256], DD[:, 3, :], ALU.mult))
            reached(dve.tensor_scalar(cv[:], cv[:], bias(3), None, ALU.add))
            tt(D10[:], DD[:, 0], DD[:, 1], ALU.mult)
            x_low(3)
            dve.wait_ge(s_in["xe"], 16)
            edge_in(0)
            def edge_step(b):
                if divmod(b, NG) in groups_edge:
                    c, k = groups_edge[divmod(b, NG)]
                    edge(c, k)
                    if k == 3 and c + 1 < B // EC:
                        edge_in(c + 1)

            for b in range(B + 1):
                g, i = divmod(b, NG)
                if b == 4:
                    edge_step(3)
                    finish(0)
                if g + 1 < NGR:
                    for k in range(7):
                        if PIECE_SLOT[k] == i - 1:
                            piece(g + 1, k)
                if b and b + 1 < B:
                    z_low(b + 1)
                if b + 2 < B:
                    z_full(b + 2)
                if b + 4 < B:
                    x_low(b + 4)
                if b != 4:
                    edge_step(b - 1)
                if b == 4:
                    finish(1)
                elif b > 4 and b % Q == 0 and b < B:
                    finish(b // Q - 1)
                if b > B - Q:
                    finish_last(b - 1 - (B - Q))



def layouts(x, cond_512, w, bia, mw, mb):
    import numpy as np
    f = np.float32
    B, C, L = x.shape
    xp = np.zeros((B, C, L + 2), f); xp[:, :, 1:L + 1] = x
    xin = np.ascontiguousarray(xp.reshape(B, C, L // 2 + 1, 2).transpose(0, 3, 1, 2)).reshape(B, 128, L // 2 + 1)
    xe = np.concatenate([xp[:, :, 0:7], xp[:, :, L - 5:L + 2]], axis=1).transpose(1, 0, 2)
    l0 = np.zeros((2, C, 2, 2, C), f)
    for j in range(2):
        for r in range(2):
            for h in range(2):
                t = 2 * j + r - h
                if 0 <= t < 3: l0[r, :, j, h, :] = w[0, :, :, t].T
    a2 = np.zeros((2, C, 8, C), f)
    for s in range(4):
        a2[:, :, 4 + s, :] = w[2, :, :, min(s, 2)]
    for s in range(4):
        for r in range(2):
            if 0 <= s - r < 3: a2[r, :, s, :] = w[2, :, :, s - r]
    b1 = np.zeros((2, C, 14, C), f)
    for s in range(-2, 12):
        for r in range(2):
            if 0 <= s - r < 3: b1[r, :, s + 2, :] = w[1, :, :, 2 - (s - r)].T
    q3 = np.zeros((2, C, 2, C), f)
    for p in range(2):
        for r in range(2):
            q3[r, :, p, :] = w[3, :, :, min(2 * p + r, 2)].T
    ed = np.zeros((2, C, 4, 3, 2, C), f)
    for s in range(2):
        ed[s, :, :, :, s, :] = w.transpose(2, 0, 3, 1)
        ed[s, :, 1, :, s, :] = w[1].transpose(0, 2, 1)
    wt = w.transpose(2, 0, 3, 1)
    wt = np.stack([wt, wt], axis=3)
    mwt = np.stack([mw.transpose(2, 0, 1)] * 2, axis=2)
    bb = np.stack([bia.T, mb.T], axis=1)
    bb = np.concatenate([bb, bb], axis=0)
    out = dict(xin=xin, xe=xe, l0=l0.reshape(128, 256), a2=a2.reshape(128, 512), b1=b1.reshape(128, 14 * 64),
               q3=q3.reshape(128, 128), ed=ed.reshape(128, 12 * 128), wt=wt.reshape(64, 12 * 128),
               mwt=mwt.reshape(128, 512), bb=bb.reshape(128, 8), st=cond_512.T)
    return {k: np.ascontiguousarray(v) for k, v in out.items()}


_ORDER = ["xin", "xe", "l0", "a2", "b1", "q3", "ed", "wt", "mwt", "bb", "st"]


def kernel(x, cond_512, L0_cond_weights, L0_cond_biases, L0_cond_mod_w, L0_cond_mod_b):
    import numpy as np
    import concourse.bacc as bacc
    from concourse.bass_utils import run_bass_kernel_spmd

    d = layouts(*(np.asarray(a) for a in (x, cond_512, L0_cond_weights, L0_cond_biases, L0_cond_mod_w,
                                          L0_cond_mod_b)))
    d["xe"] = d["xe"].reshape(128, B, 7)
    nc = bacc.Bacc("TRN2", target_bir_lowering=False, num_devices=1)
    arrays = {f"in_{n}": d[n] for n in _ORDER}
    args = [nc.dram_tensor(f"in_{n}", d[n].shape, F32, kind="ExternalInput").ap() for n in _ORDER]
    out = nc.dram_tensor("out_0", (B, 128, K), F32, kind="ExternalOutput").ap()
    build(nc, *args, out)
    r = run_bass_kernel_spmd(nc, [arrays], core_ids=[0])
    o = r.results[0]["out_0"].reshape(B, 2, C, K).transpose(0, 2, 3, 1).reshape(B, C, 2 * K)
    return np.ascontiguousarray(o[:, :, 1:2 * K - 1])
```
